# Optimizing a Trainium2 kernel written in Bass

```python
import numpy as np
import jax
import jax.numpy as jnp

def _softmax(x, axis=-1):
    return jax.nn.softmax(x, axis=axis)

def _gelu(x):
    return jax.nn.gelu(x, approximate=True)

def _silu(x):
    return jax.nn.silu(x)

def _sigmoid(x):
    return jax.nn.sigmoid(x)

def _layernorm(x, axis=-1, eps=1e-05):
    m = jnp.mean(x, axis=axis, keepdims=True)
    v = jnp.var(x, axis=axis, keepdims=True)
    return (x - m) / jnp.sqrt(v + eps)

def _scatter_add(tgt, idx, src, axis=0):
    return tgt.at[idx].add(src)

def _segment_sum(src, seg, n):
    return jax.ops.segment_sum(src, seg, n)
kernel_name = 'mk_rec_standalone_d1_rec_r8_3a40f9'

def setup_inputs(seed: int=0):
    np.random.seed(seed)
    _w = jnp.asarray

    def _rec_inputs():
        import jax
        import jax.numpy as jnp
        _rk = jax.random.key(seed)
        r_items = jnp.stack([jax.random.randint(jax.random.fold_in(jax.random.fold_in(_rk, 1), 0), (1024,), 1636, 295180, jnp.int32), jax.random.randint(jax.random.fold_in(jax.random.fold_in(_rk, 1), 1), (1024,), 472, 299964, jnp.int32), jax.random.randint(jax.random.fold_in(jax.random.fold_in(_rk, 1), 2), (1024,), 353, 299933, jnp.int32), jax.random.randint(jax.random.fold_in(jax.random.fold_in(_rk, 1), 3), (1024,), 1271, 299724, jnp.int32), jax.random.randint(jax.random.fold_in(jax.random.fold_in(_rk, 1), 4), (1024,), 557, 299438, jnp.int32), jax.random.randint(jax.random.fold_in(jax.random.fold_in(_rk, 1), 5), (1024,), 1609, 299052, jnp.int32), jax.random.randint(jax.random.fold_in(jax.random.fold_in(_rk, 1), 6), (1024,), 39, 298298, jnp.int32), jax.random.randint(jax.random.fold_in(jax.random.fold_in(_rk, 1), 7), (1024,), 77, 299979, jnp.int32), jax.random.randint(jax.random.fold_in(jax.random.fold_in(_rk, 1), 8), (1024,), 104, 297110, jnp.int32), jax.random.randint(jax.random.fold_in(jax.random.fold_in(_rk, 1), 9), (1024,), 1043, 298479, jnp.int32), jax.random.randint(jax.random.fold_in(jax.random.fold_in(_rk, 1), 10), (1024,), 982, 299982, jnp.int32), jax.random.randint(jax.random.fold_in(jax.random.fold_in(_rk, 1), 11), (1024,), 609, 299062, jnp.int32), jax.random.randint(jax.random.fold_in(jax.random.fold_in(_rk, 1), 12), (1024,), 497, 298826, jnp.int32), jax.random.randint(jax.random.fold_in(jax.random.fold_in(_rk, 1), 13), (1024,), 210, 297759, jnp.int32), jax.random.randint(jax.random.fold_in(jax.random.fold_in(_rk, 1), 14), (1024,), 1210, 298783, jnp.int32), jax.random.randint(jax.random.fold_in(jax.random.fold_in(_rk, 1), 15), (1024,), 160, 37447, jnp.int32), jax.random.randint(jax.random.fold_in(jax.random.fold_in(_rk, 1), 16), (1024,), 2290, 297085, jnp.int32), jax.random.randint(jax.random.fold_in(jax.random.fold_in(_rk, 1), 17), (1024,), 731, 297948, jnp.int32), jax.random.randint(jax.random.fold_in(jax.random.fold_in(_rk, 1), 18), (1024,), 232, 299091, jnp.int32), jax.random.randint(jax.random.fold_in(jax.random.fold_in(_rk, 1), 19), (1024,), 202, 299668, jnp.int32), jax.random.randint(jax.random.fold_in(jax.random.fold_in(_rk, 1), 20), (1024,), 1074, 297239, jnp.int32), jax.random.randint(jax.random.fold_in(jax.random.fold_in(_rk, 1), 21), (1024,), 481, 299257, jnp.int32), jax.random.randint(jax.random.fold_in(jax.random.fold_in(_rk, 1), 22), (1024,), 2053, 299123, jnp.int32), jax.random.randint(jax.random.fold_in(jax.random.fold_in(_rk, 1), 23), (1024,), 883, 37292, jnp.int32), jax.random.randint(jax.random.fold_in(jax.random.fold_in(_rk, 1), 24), (1024,), 202, 299637, jnp.int32), jax.random.randint(jax.random.fold_in(jax.random.fold_in(_rk, 1), 25), (1024,), 1397, 299418, jnp.int32), jax.random.randint(jax.random.fold_in(jax.random.fold_in(_rk, 1), 26), (1024,), 983, 298062, jnp.int32), jax.random.randint(jax.random.fold_in(jax.random.fold_in(_rk, 1), 27), (1024,), 88, 299428, jnp.int32), jax.random.randint(jax.random.fold_in(jax.random.fold_in(_rk, 1), 28), (1024,), 2043, 299471, jnp.int32), jax.random.randint(jax.random.fold_in(jax.random.fold_in(_rk, 1), 29), (1024,), 1142, 299225, jnp.int32), jax.random.randint(jax.random.fold_in(jax.random.fold_in(_rk, 1), 30), (1024,), 1436, 37138, jnp.int32), jax.random.randint(jax.random.fold_in(jax.random.fold_in(_rk, 1), 31), (1024,), 2996, 299779, jnp.int32), jax.random.randint(jax.random.fold_in(jax.random.fold_in(_rk, 1), 32), (1024,), 1264, 37372, jnp.int32), jax.random.randint(jax.random.fold_in(jax.random.fold_in(_rk, 1), 33), (1024,), 158, 299038, jnp.int32), jax.random.randint(jax.random.fold_in(jax.random.fold_in(_rk, 1), 34), (1024,), 413, 298759, jnp.int32), jax.random.randint(jax.random.fold_in(jax.random.fold_in(_rk, 1), 35), (1024,), 141, 299742, jnp.int32), jax.random.randint(jax.random.fold_in(jax.random.fold_in(_rk, 1), 36), (1024,), 876, 299699, jnp.int32), jax.random.randint(jax.random.fold_in(jax.random.fold_in(_rk, 1), 37), (1024,), 722, 299770, jnp.int32), jax.random.randint(jax.random.fold_in(jax.random.fold_in(_rk, 1), 38), (1024,), 1849, 298943, jnp.int32), jax.random.randint(jax.random.fold_in(jax.random.fold_in(_rk, 1), 39), (1024,), 426, 298426, jnp.int32), jax.random.randint(jax.random.fold_in(jax.random.fold_in(_rk, 1), 40), (1024,), 895, 299733, jnp.int32), jax.random.randint(jax.random.fold_in(jax.random.fold_in(_rk, 1), 41), (1024,), 252, 299290, jnp.int32), jax.random.randint(jax.random.fold_in(jax.random.fold_in(_rk, 1), 42), (1024,), 514, 299914, jnp.int32), jax.random.randint(jax.random.fold_in(jax.random.fold_in(_rk, 1), 43), (1024,), 232, 299994, jnp.int32), jax.random.randint(jax.random.fold_in(jax.random.fold_in(_rk, 1), 44), (1024,), 1524, 298860, jnp.int32), jax.random.randint(jax.random.fold_in(jax.random.fold_in(_rk, 1), 45), (1024,), 341, 299518, jnp.int32), jax.random.randint(jax.random.fold_in(jax.random.fold_in(_rk, 1), 46), (1024,), 174, 299723, jnp.int32), jax.random.randint(jax.random.fold_in(jax.random.fold_in(_rk, 1), 47), (1024,), 71, 37310, jnp.int32), jax.random.randint(jax.random.fold_in(jax.random.fold_in(_rk, 1), 48), (1024,), 5983, 299605, jnp.int32), jax.random.randint(jax.random.fold_in(jax.random.fold_in(_rk, 1), 49), (1024,), 162, 299742, jnp.int32)], axis=1)
        r_alias_inputs = jax.random.randint(jax.random.fold_in(_rk, 2), (1024, 50), 0, 50, jnp.int32)
        return (r_items, r_alias_inputs)
    r_items, r_alias_inputs = _rec_inputs()

    def _L0_rec_setup():
        import jax, jax.numpy as jnp
        import numpy as np
        NUM_NODE = 37500
        DIM = 128
        LAYERS = 2
        W_K = 12.0
        LEN_SESSION = 50
        BATCH = 256
        N_EDGES = 450000
        EPS = 1e-12

        def _global_item_conv(emb, rows, cols, vals, layers):
            n = emb.shape[0]
            h = emb
            acc = emb
            for _ in range(layers):
                h = jax.ops.segment_sum(vals[:, None] * h[cols], rows, num_segments=n)
                acc = acc + h
            return acc / (layers + 1)

        def _normalize(x):
            return x / jnp.maximum(jnp.linalg.norm(x, axis=-1, keepdims=True), EPS)
        key = jax.random.key(seed)
        ks = jax.random.split(key, 10)
        item_emb = jax.random.normal(ks[0], (NUM_NODE + 1, DIM), jnp.float32) * 0.02
        item_emb = item_emb.at[0].set(0.0)
        dst = jax.random.randint(ks[1], (N_EDGES,), 0, NUM_NODE + 1)
        src = jax.random.randint(ks[2], (N_EDGES,), 0, NUM_NODE + 1)
        adj_indices = jnp.stack([dst, src]).astype(jnp.int64)
        adj_values = jax.random.uniform(ks[3], (N_EDGES,), jnp.float32) / 12.0
        items = jax.random.randint(ks[4], (BATCH, LEN_SESSION), 0, NUM_NODE + 1).astype(jnp.int64)
        inputs = jax.random.randint(ks[5], (BATCH, LEN_SESSION), 0, NUM_NODE + 1).astype(jnp.int64)
        alias_inputs = jax.random.randint(ks[6], (BATCH, LEN_SESSION), 0, LEN_SESSION).astype(jnp.int64)
        Wq = jax.random.normal(ks[7], (DIM, DIM), jnp.float32) * 0.02
        Wk = jax.random.normal(ks[8], (DIM, DIM), jnp.float32) * 0.02
        Wv = jax.random.normal(ks[9], (DIM, DIM), jnp.float32) * 0.02
        bq = jnp.zeros((DIM,), jnp.float32)
        bk = jnp.zeros((DIM,), jnp.float32)
        bv = jnp.zeros((DIM,), jnp.float32)
        return dict(item_emb=item_emb, adj_values=adj_values, Wq=Wq, bq=bq, Wk=Wk, bk=bk, Wv=Wv, bv=bv, items=items, inputs=inputs, alias_inputs=alias_inputs, adj_indices=adj_indices)
    _L0_rec_all = _L0_rec_setup()
    _L0_rec_in = {k: v for k, v in _L0_rec_all.items() if k in ('item_emb', 'adj_values', 'Wq', 'bq', 'Wk', 'bk', 'Wv', 'bv', 'inputs', 'adj_indices')}
    del _L0_rec_all
    return {'r_items': r_items, 'r_alias_inputs': r_alias_inputs, 'L0_rec_item_emb': _L0_rec_in['item_emb'], 'L0_rec_adj_values': _L0_rec_in['adj_values'], 'L0_rec_Wq': _L0_rec_in['Wq'], 'L0_rec_bq': _L0_rec_in['bq'], 'L0_rec_Wk': _L0_rec_in['Wk'], 'L0_rec_bk': _L0_rec_in['bk'], 'L0_rec_Wv': _L0_rec_in['Wv'], 'L0_rec_bv': _L0_rec_in['bv'], 'L0_rec_inputs': _L0_rec_in['inputs'], 'L0_rec_adj_indices': _L0_rec_in['adj_indices']}

def reference(r_items, r_alias_inputs, L0_rec_item_emb, L0_rec_adj_values, L0_rec_Wq, L0_rec_bq, L0_rec_Wk, L0_rec_bk, L0_rec_Wv, L0_rec_bv, L0_rec_inputs, L0_rec_adj_indices):
    import jax
    import jax.numpy as jnp

    def _L0_rec_ref(item_emb, adj_values, Wq, bq, Wk, bk, Wv, bv, items, inputs, alias_inputs, adj_indices):
        import jax, jax.numpy as jnp
        import numpy as np
        NUM_NODE = 37500
        DIM = 128
        LAYERS = 2
        W_K = 12.0
        LEN_SESSION = 50
        BATCH = 256
        N_EDGES = 450000
        EPS = 1e-12

        def _global_item_conv(emb, rows, cols, vals, layers):
            n = emb.shape[0]
            h = emb
            acc = emb
            for _ in range(layers):
                h = jax.ops.segment_sum(vals[:, None] * h[cols], rows, num_segments=n)
                acc = acc + h
            return acc / (layers + 1)

        def _normalize(x):
            return x / jnp.maximum(jnp.linalg.norm(x, axis=-1, keepdims=True), EPS)
        rows, cols = (adj_indices[0], adj_indices[1])
        g = _global_item_conv(item_emb, rows, cols, adj_values, LAYERS)
        hidden = g[items]
        seq_hidden = jnp.take_along_axis(hidden, alias_inputs[:, :, None], axis=1)
        sess = seq_hidden.sum(axis=1)
        q = sess @ Wq.T + bq
        k = seq_hidden @ Wk.T + bk
        v = seq_hidden @ Wv.T + bv
        att = jnp.einsum('bd,bld->bl', q, k) / jnp.sqrt(jnp.asarray(DIM, jnp.float32))
        w = jax.nn.softmax(att, axis=-1)
        sess_emb = jnp.einsum('bl,bld->bd', w, v)
        select = W_K * _normalize(sess_emb)
        g_norm = _normalize(g)
        scores = select @ g_norm.T
        return scores
    y = _L0_rec_ref(L0_rec_item_emb, L0_rec_adj_values, L0_rec_Wq, L0_rec_bq, L0_rec_Wk, L0_rec_bk, L0_rec_Wv, L0_rec_bv, r_items, L0_rec_inputs, r_alias_inputs, L0_rec_adj_indices)
    return y

_drawn_inputs = setup_inputs


def setup_inputs(seed=0):
    import zlib

    import numpy as np

    out = dict(_drawn_inputs(seed))
    spreads = {'L0_rec_bq': (0.0, 2.0), 'L0_rec_bk': (0.0, 2.0), 'L0_rec_bv': (0.0, 0.1)}
    factors = {'L0_rec_Wq': 200.0, 'L0_rec_Wk': 200.0, 'L0_rec_Wv': 6.216}
    for name, (base, spread) in spreads.items():
        noise = np.random.default_rng([zlib.crc32(name.encode()), seed]).standard_normal(out[name].shape)
        drawn = base * np.exp(spread * noise) if base else spread * noise
        out[name] = jnp.asarray(drawn.astype(out[name].dtype))
    for name, factor in factors.items():
        out[name] = (out[name] * factor).astype(out[name].dtype)
    return out
```

```python
from contextlib import ExitStack

import concourse.bass as bass
from concourse import mybir

F32 = mybir.dt.float32
BF16 = mybir.dt.bfloat16
I32 = mybir.dt.int32
ALU = mybir.AluOpType
ACT = mybir.ActivationFunctionType
AX = mybir.AxisListType

P = 128
N_NODES = 37501
DIM = 128
N_EDGES = 450000
SESSIONS = 1024
LENGTH = 50
EPS = 1e-12
W_K = 12.0
LAYERS = 2

BIN_NODES = 256
BINS = -(-N_NODES // BIN_NODES)
BLOCKS = BINS * BIN_NODES // P
TABLE_ROWS = BLOCKS * P
TABLE_WORDS = BLOCKS * DIM

GROUP = 3
QUARTER_COLS = 2 * GROUP
BODY_COLS = 4 * QUARTER_COLS
SORT_TURNS = -(-N_EDGES // (P * BODY_COLS))
COLS = SORT_TURNS * BODY_COLS
RECORD = 4

HIGHS = (BINS - 1) // 16 + 1
LOWS = 16
COUNT_COLS = 8
COUNT_CHUNK = COLS // 7
COUNT_GROUPS = COUNT_CHUNK // COUNT_COLS

QUARTER = 8
BODY_TILES = 4 * QUARTER
MOST_TILES = (COLS * P + BINS * (P - 1)) // P
TURNS = -(-MOST_TILES // BODY_TILES)
TILES = TURNS * BODY_TILES
TILE_COLS = -(-TILES // P)

SUM_BLOCKS = 7
SUM_CHUNKS = BLOCKS // SUM_BLOCKS
NORM_BLOCKS = 7
NORM_CHUNKS = BLOCKS // NORM_BLOCKS

SESSION_GROUPS = SESSIONS // P
PART = 10
SCORE_COLS = 1024
SCORE_TURNS = N_NODES // (4 * SCORE_COLS)
SCORE_TAIL = N_NODES - 4 * SCORE_COLS * SCORE_TURNS
assert COUNT_CHUNK * 7 == COLS and COUNT_GROUPS * COUNT_COLS == COUNT_CHUNK
assert SUM_CHUNKS * SUM_BLOCKS == BLOCKS and SUM_CHUNKS % 2 == 0
assert NORM_CHUNKS * NORM_BLOCKS == BLOCKS and NORM_CHUNKS % 2 == 0
assert SCORE_TAIL <= SCORE_COLS and HIGHS * COUNT_COLS <= P and TILE_COLS * P >= TILES


def each_turn(engine, count):
    def run(body):
        body(0)
        with engine.Fori(1, count) as i:
            body(i)
    return run


def held(engine, value):
    return value if isinstance(value, int) else engine.to_reg(value)


def wait_past(engine, semaphore, value):
    if not (isinstance(value, int) and value <= 0):
        engine.wait_ge(semaphore, value)


def bass_graph_session_scores(
    nc, emb, edge_src, edge_dst, edge_val, items, alias, wq_t, bq, wk, bk, wv_t, bv, scores
):
    sorted_edges = nc.dram_tensor("sorted_edges", [P * TILES, RECORD], I32, kind="Internal").ap()
    h1_table = nc.dram_tensor("h1_table", [TABLE_ROWS, DIM], F32, kind="Internal").ap()
    g_table = nc.dram_tensor("g_table", [TABLE_ROWS, DIM], F32, kind="Internal").ap()
    tile_places = nc.dram_tensor("tile_places", [P, TILE_COLS], I32, kind="Internal").ap()
    sorted_v = sorted_edges.rearrange("(p t) w -> p (t w)", p=P)
    emb_v = emb.rearrange("(j p) d -> p j d", p=P)
    h1_v = h1_table.rearrange("(j p) d -> p j d", p=P)
    g_v = g_table.rearrange("(j p) d -> p j d", p=P)

    ctx = ExitStack()
    with ctx:
        def sb(name, shape, dt):
            return ctx.enter_context(nc.sbuf_tensor(name, shape, dt))

        def sem(name):
            return ctx.enter_context(nc.semaphore(name))

        table = sb("table", [P, TABLE_WORDS], F32)
        table_b = table[:, :].rearrange("p (j d) -> p j d", d=DIM)
        work = sb("work", [P, 8192], F32)
        side = sb("side", [P, 4096], F32)

        def in_table(k, dt=F32, cols=COLS):
            return table[:, k * COLS:k * COLS + cols].bitcast(dt)

        src, dst, val = in_table(0, I32), in_table(1, I32), in_table(2)
        dst_ok, near = in_table(3, I32), in_table(4)
        scratch = in_table(5)
        scratch_i = in_table(5, I32)
        halves = table[:, 6 * COLS:7 * COLS].bitcast(BF16)
        high, low = halves[:, 0:COLS], halves[:, COLS:2 * COLS]
        bin_of = table[:, 7 * COLS:8 * COLS + GROUP]
        at = 8 * COLS + GROUP + 1
        is_high = [table[:, at:at + HIGHS * COUNT_CHUNK // 2].bitcast(BF16),
                   work[:, 0:HIGHS * COUNT_CHUNK // 2].bitcast(BF16)]
        at += HIGHS * COUNT_CHUNK // 2
        is_low = [table[:, at:at + LOWS * COUNT_CHUNK // 2].bitcast(BF16),
                  work[:, 4096:4096 + LOWS * COUNT_CHUNK // 2].bitcast(BF16)]
        assert at + LOWS * COUNT_CHUNK // 2 <= TABLE_WORDS
        flat_high, flat_low = is_high, is_low
        is_high = [x.rearrange("p (h c) -> p h c", h=HIGHS) for x in is_high]
        is_low = [x.rearrange("p (l c) -> p l c", l=LOWS) for x in is_low]

        in_bin = [work[:, k * 256:k * 256 + 222].bitcast(BF16)[:, 0:GROUP * BINS]
                  .rearrange("p (k b) -> p k b", k=GROUP) for k in range(2)]
        ranked = [work[:, 512 + k * 512:512 + k * 512 + GROUP * BINS]
                  .rearrange("p (k b) -> p k b", k=GROUP) for k in range(2)]

        rows = work[:, 0:4096].rearrange("p (s d) -> p s d", d=DIM)
        places = work[:, 4096:8192].rearrange("p (s n) -> p s n", n=BIN_NODES)
        tile_place = side[0:1, 0:P * TILE_COLS].bitcast(I32)

        emb_part = [work[:, k * SUM_BLOCKS * DIM:(k + 1) * SUM_BLOCKS * DIM]
                    .rearrange("p (j d) -> p j d", d=DIM) for k in range(2)]
        NW = NORM_BLOCKS * DIM
        squares = [side[:, k * NW:(k + 1) * NW].rearrange("p (j d) -> p j d", d=DIM) for k in range(2)]
        normed = [side[:, (2 + k) * NW:(3 + k) * NW].rearrange("p (j d) -> p j d", d=DIM) for k in range(2)]
        seq = work[:, 0:LENGTH * DIM].rearrange("p (l d) -> p l d", d=DIM)
        prod = work[:, LENGTH * DIM:LENGTH * DIM + PART * DIM].rearrange("p (l d) -> p l d", d=DIM)
        out_stage = [side[:, k * SCORE_COLS:(k + 1) * SCORE_COLS] for k in range(4)]

        row_i = sb("row_i", [P, BIN_NODES], I32)
        row_f = sb("row_f", [P, BIN_NODES], F32)
        row_b = sb("row_b", [P, BINS], BF16)
        part_i = sb("part_i", [P, 1], I32)
        part_f = sb("part_f", [P, 1], F32)
        part_x = sb("part_x", [P, 2], I32)
        part_xf = sb("part_xf", [P, 2], F32)
        ident = sb("ident", [P, P], F32)
        before = sb("before", [P, P], BF16)
        ones_b = sb("ones_b", [P, P], BF16)
        ones_f = sb("ones_f", [P, P], F32)
        zeros_b = sb("zeros_b", [P, P], BF16)
        tile_i = sb("tile_i", [P, TILE_COLS], I32)
        tile_f = sb("tile_f", [P, TILE_COLS], F32)
        col8_i = sb("col8_i", [P, LOWS * COUNT_COLS], I32)
        same_col = sb("same_col", [P, LOWS * COUNT_COLS], F32)
        col8_f = same_col
        same_high = sb("same_high", [P, HIGHS], F32)
        wq_sb = sb("wq_sb", [DIM, DIM], F32)
        wk_sb = sb("wk_sb", [DIM, DIM + 1], F32)
        wv_sb = sb("wv_sb", [DIM, DIM], F32)
        bq_sb = sb("bq_sb", [DIM, 1], F32)
        bv_sb = sb("bv_sb", [1, DIM], F32)

        spread, counts_masked, bin_tiles, tiles_to, first_tile, base, compared, tile_bin = (
            work[:, 2560 + k * 192:2560 + k * 192 + n]
            for k, n in enumerate((HIGHS * LOWS, LOWS * COUNT_COLS, BINS, BINS, BINS, BINS, BINS, TILE_COLS)))
        bin_tiles_i = compared.bitcast(I32)
        folded_counts = counts_masked[:, 0:LOWS]
        tile_off = sb("tile_off", [P, TILE_COLS], I32)
        pos = [sb(f"pos{q}", [P, QUARTER_COLS], I32) for q in range(4)]
        slot_of = sb("slot_of", [P, QUARTER_COLS], I32)
        tile_of = sb("tile_of", [P, QUARTER_COLS], I32)
        target = [sb(f"target{q}", [P, QUARTER_COLS], I32) for q in range(4)]
        staged = [sb(f"staged{q}", [P, QUARTER_COLS, RECORD], I32) for q in range(4)]
        edges = [sb(f"edges{q}", [P, QUARTER * RECORD], I32) for q in range(4)]
        S = SESSION_GROUPS * LENGTH
        items_f, alias_f, picked, match = (
            work[:, 4096 + k * S:4096 + (k + 1) * S] for k in range(4))
        items_i, alias_i = (work[:, 4096 + k * S:4096 + (k + 1) * S].bitcast(I32) for k in range(4, 6))
        picked_i = sb("picked_i", [P, S + LENGTH], I32)
        group_items = sb("group_items", [P, LENGTH], I32)
        sums = [sb(f"sums{k}", [P, NORM_BLOCKS], F32) for k in range(2)]
        norms = [sb(f"norms{k}", [P, NORM_BLOCKS], F32) for k in range(2)]
        small_at = (LENGTH + PART) * DIM
        sess_sum, turned, q_t, select = (work[:, small_at + k * P:small_at + (k + 1) * P] for k in range(4))
        qk = sb("qk", [P, DIM + 1], F32)
        att = sb("att", [P, LENGTH], F32)
        prob = sb("prob", [P, LENGTH], F32)
        tiny = sb("tiny", [P, 8], F32)
        select_t = sb("select_t", [P, P], F32)

        banks = ctx.enter_context(nc.psum_tensor("banks", [P, 8, 512], F32))
        GB = GROUP * BINS
        counts_ps = banks[0:HIGHS * COUNT_COLS, 0, 0:LOWS * COUNT_COLS]
        all_counts_ps = banks[:, 1, 0:HIGHS * LOWS]
        rank_ps = [banks[:, 2 + k, 0:GB].rearrange("p (k b) -> p k b", k=GROUP) for k in range(2)]
        total_ps = [banks[:, 4 + k, 0:BINS] for k in range(2)]

        def product_ps(q, k):
            return banks[:, 4 * (q % 2) + k // 2, 256 * (k % 2):256 * (k % 2) + 256]

        def pair(k):
            return banks[:, 2 * k:2 * k + 2, :].rearrange("p b n -> p (b n)")

        sess_t_ps, q_ps, qk_ps = banks[:, 6, 0:128], banks[:, 6, 128:256], banks[:, 6, 256:385]
        mix_ps, emb_ps, select_ps = banks[:, 7, 0:128], banks[:, 7, 128:256], banks[:, 7, 256:384]

        edges_loaded = sem("edges_loaded")
        items_loaded = sem("items_loaded")
        weights_loaded = sem("weights_loaded")
        patterns_made = sem("patterns_made")
        constants_made = sem("constants_made")
        dve_step = sem("dve_step")
        highs_lows_made = sem("highs_lows_made")
        counted = sem("counted")
        counts_done = sem("counts_done")
        spread_made = sem("spread_made")
        counts_spread = sem("counts_spread")
        edges_split = sem("edges_split")
        in_bin_made = sem("in_bin_made")
        ranked_by_pe = sem("ranked_by_pe")
        rank_taken = sem("rank_taken")
        rank_step = sem("rank_step")
        base_moved = sem("base_moved")
        target_ready = [sem(f"target_ready{q}") for q in range(4)]
        staged_ready = [sem(f"staged_ready{q}") for q in range(4)]
        scattered = [sem(f"scattered{q}") for q in range(4)]
        places_computed = sem("places_computed")
        places_saved = sem("places_saved")
        places_back = sem("places_back")
        table_ready = sem("table_ready")
        edges_in = [[sem(f"edges_in{y}{q}") for q in range(4)] for y in range(LAYERS)]
        gathered = [[sem(f"gathered{y}{q}") for q in range(4)] for y in range(LAYERS)]
        weights_made = [[sem(f"weights_made{y}{q}") for q in range(4)] for y in range(LAYERS)]
        products = [[sem(f"products{y}{q}") for q in range(4)] for y in range(LAYERS)]
        folded = [[sem(f"folded{y}{q}") for q in range(4)] for y in range(LAYERS)]
        folds = [sem(f"folds{y}") for y in range(LAYERS)]
        h1_written = sem("h1_written")
        items_picked = sem("items_picked")
        pick_step = sem("pick_step")
        emb_in = [sem(f"emb_in{k}") for k in range(2)]
        emb_added = [sem(f"emb_added{k}") for k in range(2)]
        g_scaled = [sem(f"g_scaled{k}") for k in range(2)]
        g_written = sem("g_written")
        squared = [sem(f"squared{k}") for k in range(2)]
        summed = [sem(f"summed{k}") for k in range(2)]
        rooted = [sem(f"rooted{k}") for k in range(2)]
        norm_step = sem("norm_step")
        normalized = [sem(f"normalized{k}") for k in range(2)]
        g_turned = [sem(f"g_turned{k}") for k in range(2)]
        g_placed = [sem(f"g_placed{k}") for k in range(2)]
        indices_ready = sem("indices_ready")
        seq_in = sem("seq_in")
        sess_step = sem("sess_step")
        sess_pe = sem("sess_pe")
        sess_act = sem("sess_act")
        select_ready = sem("select_ready")
        scored = [sem(f"scored{k}") for k in range(4)]
        taken = [sem(f"taken{k}") for k in range(4)]
        stored = [sem(f"stored{k}") for k in range(4)]

        block = ctx.enter_context(nc.Block())

        @block.sync
        def _(sp):
            sp.dma_start(dst, edge_dst).then_inc(edges_loaded, 16)
            sp.dma_start(src, edge_src).then_inc(edges_loaded, 16)
            sp.dma_start(val, edge_val).then_inc(edges_loaded, 16)
            sp.dma_start(wq_sb[:, :], wq_t).then_inc(weights_loaded, 16)
            sp.dma_start(wk_sb[:, 0:DIM], wk).then_inc(weights_loaded, 16)
            sp.dma_start(wk_sb[:, DIM:DIM + 1], bk).then_inc(weights_loaded, 16)
            sp.dma_start(wv_sb[:, :], wv_t).then_inc(weights_loaded, 16)
            sp.dma_start(bq_sb[:, :], bq).then_inc(weights_loaded, 16)
            sp.dma_start(bv_sb[:, :], bv).then_inc(weights_loaded, 16)
            sp.wait_ge(constants_made, 1)
            for k in range(5):
                width = TILES * RECORD // 5
                sp.dma_start(sorted_v[:, k * width:(k + 1) * width],
                             work[:, 0:width].bitcast(I32)).then_inc(h1_written, 16)

            sp.wait_ge(places_computed, 1)
            sp.dma_start(tile_places, tile_off[:, :]).then_inc(places_saved, 16)
            sp.wait_ge(places_saved, 16)
            sp.dma_start(tile_place, tile_places.rearrange("p c -> (p c)")[None, :]).then_inc(places_back, 16)

            for q in range(4):
                sp.wait_ge(scattered[q], 16 * QUARTER_COLS * SORT_TURNS)

            def load_edges(y):
                @each_turn(sp, TURNS)
                def _(i):
                    rows_before = held(sp, i * (16 * QUARTER))
                    for q in range(4):
                        sp.wait_ge(scattered[3], 16 * QUARTER_COLS * SORT_TURNS)
                        wait_past(sp, gathered[y][q], rows_before)
                        wait_past(sp, weights_made[y][q], i)
                        sp.dma_start(edges[q][:, :], sorted_v[:, bass.ds(
                            i * (BODY_TILES * RECORD) + q * QUARTER * RECORD, QUARTER * RECORD)]
                        ).then_inc(edges_in[y][q], 16)

            load_edges(0)
            for q in range(4):
                sp.wait_ge(products[0][q], TURNS)
            sp.dma_start(items_i.rearrange("p (g l) -> p g l", l=LENGTH),
                         items.rearrange("(g p) l -> p g l", p=P)).then_inc(items_loaded, 16)
            sp.dma_start(alias_i.rearrange("p (g l) -> p g l", l=LENGTH),
                         alias.rearrange("(g p) l -> p g l", p=P)).then_inc(items_loaded, 16)
            sp.wait_ge(folded[0][3], TURNS)
            sp.dma_start(h1_v, table_b).then_inc(h1_written, 16)
            sp.wait_ge(gathered[0][3], 16 * QUARTER * TURNS)
            load_edges(1)

            sp.wait_ge(folded[1][3], TURNS)
            @each_turn(sp, SUM_CHUNKS // 2)
            def _(i):
                for k in range(2):
                    wait_past(sp, g_scaled[k], i)
                    sp.dma_start(emb_part[k], emb_v[:, bass.ds(i * (2 * SUM_BLOCKS) + k * SUM_BLOCKS, SUM_BLOCKS), :]
                                 ).then_inc(emb_in[k], 16)
            for k in range(2):
                sp.wait_ge(g_scaled[k], SUM_CHUNKS // 2)
            sp.dma_start(g_v, table_b).then_inc(g_written, 16)

            @each_turn(sp, SESSION_GROUPS)
            def _(g):
                @each_turn(sp, SCORE_TURNS)
                def _(i):
                    for k in range(4):
                        sp.wait_ge(taken[k], g * (SCORE_TURNS + (k == 0)) + i + 1)
                        sp.dma_start(scores[bass.ds(g * P, P), bass.ds(i * (4 * SCORE_COLS) + k * SCORE_COLS, SCORE_COLS)],
                                     out_stage[k]).then_inc(stored[k], 16)
                sp.wait_ge(taken[0], (g + 1) * (SCORE_TURNS + 1))
                sp.dma_start(scores[bass.ds(g * P, P), 4 * SCORE_COLS * SCORE_TURNS:N_NODES],
                             out_stage[0][:, 0:SCORE_TAIL]).then_inc(stored[0], 16)
            for k in range(4):
                sp.wait_ge(stored[k], 16 * SESSION_GROUPS * (SCORE_TURNS + (k == 0)))

        @block.gpsimd
        def _(pool):
            pool.iota(row_i[:, :], [[1, BIN_NODES]], base=0, channel_multiplier=0).then_inc(patterns_made, 1)
            pool.iota(part_i[:, :], [[0, 1]], base=0, channel_multiplier=1).then_inc(patterns_made, 1)
            pool.iota(tile_i[:, :], [[1, TILE_COLS]], base=0, channel_multiplier=TILE_COLS).then_inc(patterns_made, 1)
            pool.iota(col8_i[:, :], [[0, LOWS], [1, COUNT_COLS]], base=0, channel_multiplier=0).then_inc(patterns_made, 1)

            @each_turn(pool, SORT_TURNS)
            def _(i):
                turn = held(pool, i + 1)
                for q in range(4):
                    pool.wait_ge(h1_written, 16 * 5)
                    pool.wait_ge(target_ready[q], turn)
                    pool.wait_ge(staged_ready[q], turn)
                    for c in range(QUARTER_COLS):
                        pool.indirect_dma_start(
                            sorted_edges, bass.IndirectOffsetOnAxis(target[q][:, c:c + 1], 0),
                            staged[q][:, c, :], None,
                        ).then_inc(scattered[q], 16)

            def gather_rows(y, source):
                @each_turn(pool, TURNS)
                def _(i):
                    edges_so_far = held(pool, (i + 1) * 16)
                    for q in range(4):
                        pool.wait_ge(h1_written, 16 * (5 + y))
                        pool.wait_ge(edges_in[y][q], edges_so_far)
                        wait_past(pool, products[y][q], i)
                        for t in range(QUARTER):
                            pool.indirect_dma_start(
                                rows[:, q * QUARTER + t, :], None, source,
                                bass.IndirectOffsetOnAxis(edges[q][:, t * RECORD:t * RECORD + 1], 0),
                            ).then_inc(gathered[y][q], 16)

            gather_rows(0, emb)
            gather_rows(1, h1_table)

            @each_turn(pool, SESSION_GROUPS)
            def _(g):
                groups, steps_before = held(pool, g + 1), held(pool, g * 6)
                pool.wait_ge(g_written, 16)
                pool.wait_ge(indices_ready, groups)
                wait_past(pool, sess_pe, steps_before)
                for l in range(LENGTH):
                    pool.indirect_dma_start(
                        seq[:, l, :], None, g_table,
                        bass.IndirectOffsetOnAxis(group_items[:, l:l + 1], 0),
                    ).then_inc(seq_in, 16)

        @block.tensor
        def _(pe):
            pe.wait_ge(constants_made, 3)
            HC, LC = HIGHS * COUNT_COLS, LOWS * COUNT_COLS
            pe.matmul(counts_ps, zeros_b[:, 0:HC], zeros_b[:, 0:LC], start=True, stop=False, skip_group_check=True)

            def count(k, uses):
                wait_past(pe, highs_lows_made, uses)
                for c in range(COUNT_GROUPS):
                    last = pe.matmul(counts_ps, flat_high[k][:, c::COUNT_GROUPS], flat_low[k][:, c::COUNT_GROUPS],
                                     start=False, stop=False, skip_group_check=True)
                last.then_inc(counted, 1)

            @each_turn(pe, 3)
            def _(i):
                count(0, i * 2 + 1)
                count(1, i * 2 + 2)
            count(0, 7)
            pe.matmul(counts_ps, zeros_b[:, 0:HC], zeros_b[:, 0:LC], start=False, stop=True,
                      skip_group_check=True).then_inc(counts_done, 1)
            pe.wait_ge(spread_made, 1)
            pe.matmul(all_counts_ps, ones_f[0:HC, :], spread[0:HC, :], start=True, stop=True).then_inc(counts_spread, 1)

            @each_turn(pe, SORT_TURNS)
            def _(i):
                for c in range(8):
                    k = c % 2
                    pe.wait_ge(in_bin_made, i * 8 + c + 1)
                    wait_past(pe, rank_taken, i * 8 + c - 1)
                    o = in_bin[k]
                    pe.matmul(rank_ps[k], before[:, :], o, start=True, stop=False, skip_group_check=True)
                    pe.matmul(rank_ps[k][:, 1:3, :], ones_b[:, :],
                              o[:, 0:1, :].to_broadcast([P, 2, BINS]), start=False, stop=False, skip_group_check=True)
                    pe.matmul(rank_ps[k][:, 2:3, :], ones_b[:, :], o[:, 1:2, :], start=False, stop=True, skip_group_check=True)
                    for x in range(GROUP):
                        last = pe.matmul(total_ps[k], ones_b[:, :], o[:, x, :], start=(x == 0), stop=(x == GROUP - 1))
                    last.then_inc(ranked_by_pe, 1)

            def layer(y):
                @each_turn(pe, TURNS)
                def _(i):
                    for q in range(4):
                        pe.wait_ge(gathered[y][q], (i + 1) * (16 * QUARTER))
                        pe.wait_ge(weights_made[y][q], i + 1)
                        wait_past(pe, folded[y][(q + 2) % 4], i + (q >= 2))
                        for t in range(QUARTER):
                            for h in range(2):
                                last = pe.matmul(
                                    product_ps(q, t)[:, h * DIM:(h + 1) * DIM],
                                    places[:, (q % 2) * QUARTER + t, h * P:(h + 1) * P],
                                    rows[:, q * QUARTER + t, :], start=True, stop=True)
                        last.then_inc(products[y][q], 1)

            layer(0)
            layer(1)

            pe.wait_ge(folded[1][3], TURNS)
            @each_turn(pe, NORM_CHUNKS // 2)
            def _(i):
                for k in range(2):
                    pe.wait_ge(normalized[k], i + 1)
                    wait_past(pe, g_placed[k], i * 2)
                    for j in range(NORM_BLOCKS):
                        last = pe.transpose(banks[:, 2 * k + j // 4, (j % 4) * P:(j % 4 + 1) * P],
                                            normed[k][:, j, :], ident[:, :])
                    last.then_inc(g_turned[k], 1)

            pe.wait_ge(weights_loaded, 16 * 6)
            for k in range(2):
                pe.wait_ge(g_placed[k], NORM_CHUNKS)
            @each_turn(pe, SESSION_GROUPS)
            def _(g):
                wait_past(pe, taken[3], g * SCORE_TURNS)
                pe.wait_ge(sess_step, g * 9 + 1)
                pe.transpose(sess_t_ps, sess_sum, ident[:, :]).then_inc(sess_pe, 1)
                pe.wait_ge(sess_step, g * 9 + 2)
                pe.matmul(q_ps, wq_sb[:, :], turned, start=True, stop=True).then_inc(sess_pe, 1)
                pe.wait_ge(sess_act, g * 4 + 1)
                pe.matmul(qk_ps, q_t, wk_sb[:, :], start=True, stop=True).then_inc(sess_pe, 1)
                pe.wait_ge(sess_step, g * 9 + 6)
                for l in range(LENGTH):
                    last = pe.matmul(mix_ps, seq[:, l, :], ident[:, :], start=(l == 0), stop=(l == LENGTH - 1))
                last.then_inc(sess_pe, 1)
                pe.wait_ge(sess_step, g * 9 + 7)
                pe.matmul(emb_ps, turned, wv_sb[:, :], start=True, stop=False)
                pe.matmul(emb_ps, ones_f[0:1, :], bv_sb[:, :], start=False, stop=True).then_inc(sess_pe, 1)
                pe.wait_ge(sess_step, g * 9 + 8)
                pe.transpose(select_ps, select, ident[:, :]).then_inc(sess_pe, 1)

                def score(k, uses, col, width):
                    wait_past(pe, taken[k], uses)
                    for h in range(-(-width // 512)):
                        w = min(512, width - 512 * h)
                        last = pe.matmul(banks[:, 2 * k + h, 0:w], select_t[:, :],
                                         table[:, bass.ds(col + 512 * h, w)], start=True, stop=True)
                    last.then_inc(scored[k], 1)

                @each_turn(pe, SCORE_TURNS)
                def _(i):
                    pe.wait_ge(sess_step, g * 9 + 9)
                    for k in range(4):
                        score(k, g * (SCORE_TURNS + (k == 0)) + i, i * (4 * SCORE_COLS) + k * SCORE_COLS, SCORE_COLS)
                score(0, g * (SCORE_TURNS + 1) + SCORE_TURNS, 4 * SCORE_COLS * SCORE_TURNS, SCORE_TAIL)

        @block.scalar
        def _(act):
            act.wait_ge(edges_split, 1)
            @each_turn(act, SORT_TURNS)
            def _(i):
                for q in range(4):
                    wait_past(act, scattered[q], i * (16 * QUARTER_COLS))
                    cols = bass.ds(i * BODY_COLS + q * QUARTER_COLS, QUARTER_COLS)
                    act.copy(staged[q][:, :, 0], src[:, cols])
                    act.copy(staged[q][:, :, 1].bitcast(F32), near[:, cols])
                    act.copy(staged[q][:, :, 2].bitcast(F32), val[:, cols]).then_inc(staged_ready[q], 1)

            @each_turn(act, SUM_CHUNKS // 2)
            def _(i):
                for k in range(2):
                    act.wait_ge(emb_added[k], i + 1)
                    act.mul(table_b[:, bass.ds(i * (2 * SUM_BLOCKS) + k * SUM_BLOCKS, SUM_BLOCKS), :],
                            emb_part[k], 1.0 / (LAYERS + 1)).then_inc(g_scaled[k], 1)

            for k in range(2):
                act.wait_ge(g_scaled[k], SUM_CHUNKS // 2)

            def group_indices(g):
                act.copy(group_items[:, :], picked_i[:, bass.ds(g * LENGTH, LENGTH)]).then_inc(indices_ready, 1)

            act.wait_ge(items_picked, 2)
            group_indices(0)

            @each_turn(act, NORM_CHUNKS // 2)
            def _(i):
                for k in range(2):
                    wait_past(act, summed[k], i)
                    blocks = bass.ds(i * (2 * NORM_BLOCKS) + k * NORM_BLOCKS, NORM_BLOCKS)
                    act.activation(squares[k], table_b[:, blocks, :], ACT.Square).then_inc(squared[k], 1)
                    act.wait_ge(summed[k], i + 1)
                    act.activation(norms[k][:, :], sums[k][:, :], ACT.Sqrt).then_inc(rooted[k], 1)
                    act.wait_ge(g_turned[k], i + 1)
                    act.wait_ge(g_written, 16)
                    at = i * (2 * NORM_BLOCKS * P) + k * NORM_BLOCKS * P
                    act.copy(table[:, bass.ds(at, 4 * P)], banks[:, 2 * k, :]).then_inc(g_placed[k], 1)

            @each_turn(act, SESSION_GROUPS)
            def _(g):
                act.wait_ge(sess_pe, g * 6 + 2)
                act.activation(q_t, q_ps, ACT.Identity, bias=bq_sb[:, :]).then_inc(sess_act, 1)
                act.wait_ge(seq_in, (g + 1) * (16 * LENGTH))
                act.wait_ge(sess_step, g * 9 + 5)
                act.activation(prob[:, :], att[:, :], ACT.Exp, bias=tiny[:, 0:1],
                               accum_out=tiny[:, 1:2]).then_inc(sess_act, 1)
                act.copy(group_items[:, :], picked_i[:, bass.ds((g + 1) * LENGTH, LENGTH)]).then_inc(indices_ready, 1)
                act.wait_ge(sess_pe, g * 6 + 5)
                act.activation(q_t, emb_ps, ACT.Square, accum_out=tiny[:, 3:4]).then_inc(sess_act, 1)
                act.wait_ge(sess_act, g * 4 + 3)
                act.activation(tiny[:, 4:5], tiny[:, 3:4], ACT.Sqrt).then_inc(sess_act, 1)

                def take(k, uses, width):
                    act.wait_ge(scored[k], uses + 1)
                    wait_past(act, stored[k], uses * 16)
                    act.copy(out_stage[k][:, 0:width], pair(k)[:, 0:width]).then_inc(taken[k], 1)

                @each_turn(act, SCORE_TURNS)
                def _(i):
                    for k in (0, 2):
                        take(k, g * (SCORE_TURNS + (k == 0)) + i, SCORE_COLS)
                take(0, g * (SCORE_TURNS + 1) + SCORE_TURNS, SCORE_TAIL)

        @block.vector
        def _(dve):
            steps = [0]

            def done(instruction):
                steps[0] += 1
                instruction.then_inc(dve_step, 1)
                dve.wait_ge(dve_step, steps[0])

            dve.memset(work[:, :], 0.0).then_inc(constants_made, 1)
            dve.memset(ones_b[:, :], 1.0).then_inc(constants_made, 1)
            dve.memset(zeros_b[:, :], 0.0).then_inc(constants_made, 1)
            done(dve.memset(ones_f[:, :], 1.0))
            done(dve.memset(bin_of[:, COLS:COLS + GROUP], 0.0))
            for q in range(4):
                done(dve.memset(staged[q][:, :, :], 0))
            dve.wait_ge(patterns_made, 4)
            done(dve.tensor_copy(row_f[:, :], row_i[:, :]))
            done(dve.tensor_copy(part_f[:, :], part_i[:, :]))
            done(dve.tensor_copy(tile_f[:, :], tile_i[:, :]))
            done(dve.tensor_copy(row_b[:, :], row_f[:, 0:BINS]))
            done(dve.tensor_scalar(ident[:, :], row_f[:, 0:P], part_f[:, 0:1], None, ALU.is_equal))
            done(dve.tensor_scalar(before[:, :], row_f[:, 0:P], part_f[:, 0:1], None, ALU.is_gt))
            done(dve.tensor_scalar(part_x[:, 0:1], part_i[:, :], COUNT_COLS - 1, None, ALU.bitwise_and))
            done(dve.tensor_scalar(part_x[:, 1:2], part_i[:, :], 3, None, ALU.logical_shift_right))
            done(dve.tensor_copy(part_xf[:, :], part_x[:, :]))
            done(dve.tensor_copy(col8_f[:, :], col8_i[:, :]))
            done(dve.tensor_scalar(same_col[:, :], col8_f[:, :], part_xf[:, 0:1], None, ALU.is_equal))
            done(dve.tensor_scalar(same_high[:, :], row_f[:, 0:HIGHS], part_xf[:, 1:2], None, ALU.is_equal))

            dve.wait_ge(edges_loaded, 48)
            done(dve.tensor_scalar(dst_ok, dst, 0.0, float(N_NODES - 1), ALU.max, ALU.min))
            done(dve.tensor_scalar(scratch_i, dst_ok, 12, None, ALU.logical_shift_right))
            done(dve.tensor_copy(high, scratch_i))
            done(dve.tensor_scalar(scratch_i, dst_ok, 8, LOWS - 1, ALU.logical_shift_right, ALU.bitwise_and))
            done(dve.tensor_copy(low, scratch_i))

            def highs_lows(k, col):
                for h in range(HIGHS):
                    dve.tensor_scalar(is_high[k][:, h, :], high[:, bass.ds(col, COUNT_CHUNK)], float(h), None,
                                      ALU.is_equal)
                for l in range(LOWS):
                    last = dve.tensor_scalar(is_low[k][:, l, :], low[:, bass.ds(col, COUNT_CHUNK)], float(l), None,
                                             ALU.is_equal)
                last.then_inc(highs_lows_made, 1)

            dve.wait_ge(h1_written, 16 * 5)
            highs_lows(0, 0)
            @each_turn(dve, 3)
            def _(i):
                wait_past(dve, counted, i * 2)
                highs_lows(1, i * (2 * COUNT_CHUNK) + COUNT_CHUNK)
                dve.wait_ge(counted, i * 2 + 1)
                highs_lows(0, i * (2 * COUNT_CHUNK) + 2 * COUNT_CHUNK)

            done(dve.tensor_tensor(scratch, dst_ok, dst, ALU.is_equal))
            done(dve.tensor_tensor(val, val, scratch, ALU.mult))
            done(dve.tensor_scalar(scratch_i, dst_ok, BIN_NODES - 1, None, ALU.bitwise_and))
            done(dve.tensor_copy(near, scratch_i))
            done(dve.tensor_scalar(scratch_i, dst_ok, 8, None, ALU.logical_shift_right))
            done(dve.tensor_copy(bin_of[:, 0:COLS], scratch_i))
            done(dve.tensor_scalar(scratch, src, 0.0, float(N_NODES), ALU.is_lt, ALU.mult))
            done(dve.tensor_tensor(src, src, scratch, ALU.add))
            dve.tensor_scalar(src, src, 0.0, float(N_NODES - 1), ALU.max, ALU.min).then_inc(edges_split, 1)

            dve.wait_ge(counts_done, 1)
            HC = HIGHS * COUNT_COLS
            done(dve.tensor_tensor(scratch[0:HC, 0:LOWS * COUNT_COLS], counts_ps, same_col[0:HC, :], ALU.mult))
            done(dve.tensor_reduce(folded_counts[0:HC, :], scratch[0:HC, 0:LOWS * COUNT_COLS].rearrange(
                "p (l c) -> p l c", l=LOWS), AX.X, ALU.add))
            dve.tensor_tensor(spread[0:HC, :].rearrange("p (h l) -> p h l", h=HIGHS),
                              same_high[0:HC, :, None].to_broadcast([HC, HIGHS, LOWS]),
                              folded_counts[0:HC, None, :].to_broadcast([HC, HIGHS, LOWS]),
                              ALU.mult).then_inc(spread_made, 1)
            dve.wait_ge(counts_spread, 1)
            done(dve.tensor_scalar(bin_tiles_i, all_counts_ps[:, 0:BINS], float(P - 1), None, ALU.add))
            done(dve.tensor_scalar(bin_tiles_i, bin_tiles_i, 7, None, ALU.logical_shift_right))
            done(dve.tensor_copy(bin_tiles, bin_tiles_i))
            done(dve.tensor_tensor_scan(tiles_to, ones_f[:, 0:1].to_broadcast([P, BINS]), bin_tiles,
                                        0.0, ALU.mult, ALU.add))
            done(dve.tensor_tensor(first_tile, tiles_to, bin_tiles, ALU.subtract))
            done(dve.tensor_scalar(base, first_tile, float(P), None, ALU.mult))

            def one_hot(k, col):
                for x in range(GROUP):
                    last = dve.tensor_scalar(in_bin[k][:, x, :], row_b[:, :], bin_of[:, bass.ds(col + x, 1)], None,
                                             ALU.is_equal)
                last.then_inc(in_bin_made, 1)

            one_hot(0, 0)
            @each_turn(dve, SORT_TURNS)
            def _(i):
                for c in range(8):
                    k, q = c % 2, c // 2
                    one_hot(1 - k, i * BODY_COLS + (c + 1) * GROUP)
                    dve.wait_ge(ranked_by_pe, i * 8 + c + 1)
                    wait_past(dve, base_moved, i * 8 + c)
                    dve.tensor_tensor(ranked[k], rank_ps[k], base[:, None, :].to_broadcast([P, GROUP, BINS]),
                                      ALU.add).then_inc(rank_step, 1)
                    dve.wait_ge(rank_step, (i * 8 + c) * 2 + 1)
                    dve.tensor_tensor(base, base, total_ps[k], ALU.add).then_inc(base_moved, 1)
                    dve.tensor_tensor(ranked[k], ranked[k], in_bin[k], ALU.mult).then_inc(rank_step, 1)
                    dve.wait_ge(rank_step, (i * 8 + c) * 2 + 2)
                    with nc.allow_low_precision(reason="positions are whole numbers below 2**24"):
                        dve.tensor_reduce(pos[q][:, k * GROUP:(k + 1) * GROUP], ranked[k], AX.X,
                                          ALU.add).then_inc(rank_taken, 1)
                    if k == 1:
                        dve.wait_ge(rank_taken, i * 8 + c + 1)
                        dve.tensor_scalar(slot_of[:, :], pos[q][:, :], P - 1, None, ALU.bitwise_and).then_inc(pick_step, 1)
                        dve.tensor_scalar(tile_of[:, :], pos[q][:, :], 7, None, ALU.logical_shift_right).then_inc(pick_step, 1)
                        dve.wait_ge(pick_step, (i * 4 + q) * 2 + 2)
                        wait_past(dve, scattered[q], i * (16 * QUARTER_COLS))
                        dve.scalar_tensor_tensor(out=target[q][:, :], in0=slot_of[:, :], scalar=float(TILES),
                                                 in1=tile_of[:, :], op0=ALU.mult, op1=ALU.add).then_inc(target_ready[q], 1)

            for c in range(TILE_COLS):
                done(dve.tensor_scalar(compared, first_tile, tile_f[:, c:c + 1], None, ALU.is_le, ALU.add,
                                       accum_out=tile_bin[:, c:c + 1]))
            dve.tensor_scalar(tile_off[:, :], tile_bin[:, :], -1.0, float(2 * DIM), ALU.add,
                              ALU.mult).then_inc(places_computed, 1)

            for q in range(4):
                dve.wait_ge(staged_ready[q], SORT_TURNS)
            done(dve.memset(table[:, :], 0.0))
            dve.wait_ge(places_back, 16)

            def weights(q, t):
                e = edges[q][:, t * RECORD:(t + 1) * RECORD].bitcast(F32)
                return dve.tensor_scalar(places[:, (q % 2) * QUARTER + t, :], row_f[:, :], e[:, 1:2], e[:, 2:3],
                                         ALU.is_equal, ALU.mult)

            def layer(y):
                def fold(i, q, ahead):
                    dve.wait_ge(products[y][q], i + 1)
                    q2 = (q + 2) % 4
                    if ahead:
                        dve.wait_ge(edges_in[y][q2], (i + 1 + (q >= 2)) * 16)
                    _, off = nc.values_load_multi_w_load_instructions(
                        tile_place[0:1, bass.ds(i * BODY_TILES + q * QUARTER, QUARTER)], engines=[dve.engine],
                        min_val=0, max_val=TABLE_WORDS - BIN_NODES,
                        skip_runtime_bounds_check_because="the places are computed on the chip, one of BINS")
                    for t in range(QUARTER):
                        into = table[:, bass.ds(off[t], 2 * DIM)]
                        if t:
                            wait_past(dve, folds[y], (i * 4 + q) * (QUARTER - 1) + t)
                        else:
                            wait_past(dve, folded[y][(q + 3) % 4], i + (q > 0))
                        dve.tensor_tensor(into, into, product_ps(q, t), ALU.add).then_inc(
                            folds[y] if t < QUARTER - 1 else folded[y][q], 1)
                        if ahead:
                            made = weights(q2, t)
                    if ahead:
                        made.then_inc(weights_made[y][q2], 1)

                for q in range(2):
                    dve.wait_ge(edges_in[y][q], 16)
                    for t in range(QUARTER):
                        made = weights(q, t)
                    made.then_inc(weights_made[y][q], 1)
                @each_turn(dve, TURNS - 1)
                def _(i):
                    for q in range(4):
                        fold(i, q, True)
                for q in range(4):
                    fold(TURNS - 1, q, q < 2)

            layer(0)

            dve.wait_ge(items_loaded, 32)
            dve.wait_ge(gathered[0][3], 16 * QUARTER * TURNS)
            for x, n, y in ((items_i, N_NODES, items_f), (alias_i, LENGTH, alias_f)):
                done(dve.tensor_scalar(y, x, 0.0, float(n), ALU.is_lt, ALU.mult))
                done(dve.tensor_tensor(y, y, x, ALU.add))
            done(dve.tensor_scalar(items_f, items_f, 0.0, float(N_NODES - 1), ALU.max, ALU.min))
            done(dve.memset(picked, 0.0))
            items_g = items_f.rearrange("p (g l) -> p g l", l=LENGTH)
            alias_g = alias_f.rearrange("p (g l) -> p g l", l=LENGTH)
            match_g = match.rearrange("p (g l) -> p g l", l=LENGTH)
            picks = SORT_TURNS * 8
            @each_turn(dve, LENGTH)
            def _(j):
                dve.wait_ge(pick_step, j * 2 + picks)
                dve.scalar_tensor_tensor(
                    out=match_g, in0=alias_g, scalar=row_f[:, bass.ds(j, 1)],
                    in1=items_g[:, :, bass.ds(j, 1)].to_broadcast([P, SESSION_GROUPS, LENGTH]),
                    op0=ALU.is_equal, op1=ALU.mult).then_inc(pick_step, 1)
                dve.wait_ge(pick_step, j * 2 + picks + 1)
                dve.tensor_tensor(picked, picked, match, ALU.add).then_inc(pick_step, 1)
            dve.wait_ge(pick_step, picks + 2 * LENGTH)
            dve.memset(picked_i[:, S:S + LENGTH], 0).then_inc(items_picked, 1)
            dve.tensor_copy(picked_i[:, 0:S], picked).then_inc(items_picked, 1)

            dve.wait_ge(h1_written, 16 * 6)
            dve.wait_ge(items_picked, 2)
            layer(1)

            dve.wait_ge(folded[1][3], TURNS)
            @each_turn(dve, SUM_CHUNKS // 2)
            def _(i):
                for k in range(2):
                    dve.wait_ge(emb_in[k], (i + 1) * 16)
                    blocks = bass.ds(i * (2 * SUM_BLOCKS) + k * SUM_BLOCKS, SUM_BLOCKS)
                    dve.tensor_tensor(emb_part[k], emb_part[k], table_b[:, blocks, :], ALU.add).then_inc(emb_added[k], 1)

            @each_turn(dve, NORM_CHUNKS // 2)
            def _(i):
                for k in range(2):
                    dve.wait_ge(squared[k], i + 1)
                    dve.tensor_reduce(sums[k][:, :], squares[k], AX.X, ALU.add).then_inc(summed[k], 1)
                    dve.wait_ge(rooted[k], i + 1)
                    dve.tensor_scalar(norms[k][:, :], norms[k][:, :], EPS, None, ALU.max).then_inc(norm_step, 1)
                    dve.wait_ge(norm_step, i * 4 + 2 * k + 1)
                    dve.reciprocal(norms[k][:, :], norms[k][:, :]).then_inc(norm_step, 1)
                    dve.wait_ge(norm_step, i * 4 + 2 * k + 2)
                    wait_past(dve, g_turned[k], i)
                    blocks = bass.ds(i * (2 * NORM_BLOCKS) + k * NORM_BLOCKS, NORM_BLOCKS)
                    dve.tensor_tensor(normed[k], table_b[:, blocks, :],
                                      norms[k][:, :, None].to_broadcast([P, NORM_BLOCKS, DIM]),
                                      ALU.mult).then_inc(normalized[k], 1)
                    dve.wait_ge(g_turned[k], i + 1)
                    dve.wait_ge(g_written, 16)
                    at = i * (2 * NORM_BLOCKS * P) + k * NORM_BLOCKS * P
                    dve.tensor_copy(table[:, bass.ds(at + 4 * P, (NORM_BLOCKS - 4) * P)],
                                    banks[:, 2 * k + 1, 0:(NORM_BLOCKS - 4) * P]).then_inc(g_placed[k], 1)

            @each_turn(dve, SESSION_GROUPS)
            def _(g):
                def step(n, instruction):
                    instruction.then_inc(sess_step, 1)
                    return n

                dve.wait_ge(seq_in, (g + 1) * (16 * LENGTH))
                step(1, dve.tensor_reduce(sess_sum, seq.rearrange("p l d -> p d l"), AX.X, ALU.add))
                dve.wait_ge(sess_pe, g * 6 + 1)
                step(2, dve.tensor_copy(turned, sess_t_ps))
                dve.wait_ge(sess_pe, g * 6 + 3)
                step(3, dve.tensor_copy(qk[:, :], qk_ps))
                dve.wait_ge(sess_step, g * 9 + 3)
                PARTS = LENGTH // PART
                for c in range(PARTS):
                    part = slice(c * PART, (c + 1) * PART)
                    dve.wait_ge(norm_step, g * (2 * PARTS + 5) + NORM_CHUNKS * 2 + 2 * c)
                    dve.tensor_tensor(prod, seq[:, part, :], qk[:, None, 0:DIM].to_broadcast([P, PART, DIM]),
                                      ALU.mult).then_inc(norm_step, 1)
                    dve.wait_ge(norm_step, g * (2 * PARTS + 5) + NORM_CHUNKS * 2 + 2 * c + 1)
                    dve.tensor_reduce(att[:, part], prod, AX.X, ALU.add).then_inc(norm_step, 1)
                more = NORM_CHUNKS * 2 + 2 * PARTS
                each = 2 * PARTS + 5
                dve.wait_ge(norm_step, g * each + more)
                step(4, dve.tensor_scalar(att[:, :], att[:, :], qk[:, DIM:DIM + 1], float(DIM) ** -0.5,
                                          ALU.add, ALU.mult))
                dve.wait_ge(sess_step, g * 9 + 4)
                dve.tensor_reduce(tiny[:, 2:3], att[:, :], AX.X, ALU.max).then_inc(norm_step, 1)
                dve.wait_ge(norm_step, g * each + more + 1)
                step(5, dve.tensor_scalar(tiny[:, 0:1], tiny[:, 2:3], -1.0, None, ALU.mult))
                dve.wait_ge(sess_act, g * 4 + 2)
                dve.reciprocal(tiny[:, 5:6], tiny[:, 1:2]).then_inc(norm_step, 1)
                dve.wait_ge(norm_step, g * each + more + 2)
                dve.tensor_scalar(prob[:, :], prob[:, :], tiny[:, 5:6], None, ALU.mult).then_inc(norm_step, 1)
                dve.wait_ge(norm_step, g * each + more + 3)
                step(6, dve.tensor_tensor(seq, seq, prob[:, :, None].to_broadcast([P, LENGTH, DIM]), ALU.mult))
                dve.wait_ge(sess_pe, g * 6 + 4)
                step(7, dve.tensor_copy(turned, mix_ps))
                dve.wait_ge(sess_act, g * 4 + 4)
                dve.tensor_scalar(tiny[:, 6:7], tiny[:, 4:5], EPS, None, ALU.max).then_inc(norm_step, 1)
                dve.wait_ge(norm_step, g * each + more + 4)
                dve.reciprocal(tiny[:, 7:8], tiny[:, 6:7]).then_inc(norm_step, 1)
                dve.wait_ge(norm_step, g * each + more + 5)
                step(8, dve.tensor_scalar(select, emb_ps, tiny[:, 7:8], W_K, ALU.mult, ALU.mult))
                dve.wait_ge(sess_pe, g * 6 + 6)
                step(9, dve.tensor_copy(select_t[:, :], select_ps))

                def take(k, uses):
                    dve.wait_ge(scored[k], uses + 1)
                    wait_past(dve, stored[k], uses * 16)
                    dve.tensor_copy(out_stage[k], pair(k)).then_inc(taken[k], 1)

                @each_turn(dve, SCORE_TURNS)
                def _(i):
                    for k in (1, 3):
                        take(k, g * SCORE_TURNS + i)


def kernel(**inputs):
    import numpy as np
    import concourse.bacc as bacc
    from concourse.bass_utils import run_bass_kernel_spmd as run

    def flat(x):
        return np.ascontiguousarray(x)

    emb = np.zeros((TABLE_ROWS, DIM), np.float32)
    emb[:N_NODES] = inputs["L0_rec_item_emb"]
    adj = np.asarray(inputs["L0_rec_adj_indices"])
    edges = np.zeros((2, P * COLS), adj.dtype)
    edges[0] = N_NODES - 1
    edges[:, :N_EDGES] = adj
    val = np.zeros(P * COLS, np.float32)
    val[:N_EDGES] = inputs["L0_rec_adj_values"]
    arrays = {
        "emb": emb,
        "edge_src": flat(edges[1].reshape(P, COLS)),
        "edge_dst": flat(edges[0].reshape(P, COLS)),
        "edge_val": val.reshape(P, COLS),
        "items": flat(inputs["r_items"]),
        "alias": flat(inputs["r_alias_inputs"]),
        "wq_t": flat(np.asarray(inputs["L0_rec_Wq"]).T),
        "bq": flat(np.asarray(inputs["L0_rec_bq"]).reshape(DIM, 1)),
        "wk": flat(inputs["L0_rec_Wk"]),
        "bk": flat(np.asarray(inputs["L0_rec_bk"]).reshape(DIM, 1)),
        "wv_t": flat(np.asarray(inputs["L0_rec_Wv"]).T),
        "bv": flat(np.asarray(inputs["L0_rec_bv"]).reshape(1, DIM)),
    }
    nc = bacc.Bacc("TRN2", target_bir_lowering=False, num_devices=1)
    named = {f"in_{k}": v for k, v in arrays.items()}
    args = [nc.dram_tensor(k, v.shape, mybir.dt.from_np(v.dtype), kind="ExternalInput").ap()
            for k, v in named.items()]
    args.append(nc.dram_tensor("out_scores", [SESSIONS, N_NODES], F32, kind="ExternalOutput").ap())
    bass_graph_session_scores(nc, *args)
    r = run(nc, [named], core_ids=[0])
    return r.results[0]["out_scores"]
```

```python
from contextlib import ExitStack

import concourse.bass as bass
from concourse import mybir

F32 = mybir.dt.float32
BF16 = mybir.dt.bfloat16
I32 = mybir.dt.int32
ALU = mybir.AluOpType
ACT = mybir.ActivationFunctionType
AX = mybir.AxisListType

P = 128
N_NODES = 37501
DIM = 128
N_EDGES = 450000
SESSIONS = 1024
LENGTH = 50
EPS = 1e-12
W_K = 12.0
LAYERS = 2

BIN_NODES = 256
BINS = -(-N_NODES // BIN_NODES)
BLOCKS = BINS * BIN_NODES // P
TABLE_ROWS = BLOCKS * P
TABLE_WORDS = BLOCKS * DIM

GROUP = 3
QUARTER_COLS = 2 * GROUP
BODY_COLS = 4 * QUARTER_COLS
SORT_TURNS = -(-N_EDGES // (P * BODY_COLS))
COLS = SORT_TURNS * BODY_COLS
RECORD = 4

HIGHS = (BINS - 1) // 16 + 1
LOWS = 16
COUNT_COLS = 8
COUNT_CHUNK = COLS // 7
COUNT_GROUPS = COUNT_CHUNK // COUNT_COLS

QUARTER = 8
BODY_TILES = 4 * QUARTER
MOST_TILES = (COLS * P + BINS * (P - 1)) // P
TURNS = -(-MOST_TILES // BODY_TILES)
TILES = TURNS * BODY_TILES
TILE_COLS = -(-TILES // P)

EMB_BLOCKS = 3
EMB_TURNS = BLOCKS // EMB_BLOCKS

NORM_BLOCKS = 7
NORM_CHUNKS = BLOCKS // NORM_BLOCKS

SESSION_GROUPS = SESSIONS // P
PART = 10
PARTS = LENGTH // PART
SCORE_COLS = 1024
SCORE_SLOTS = 3
TURN_COLS = SCORE_SLOTS * SCORE_COLS
SCORE_TURNS = N_NODES // TURN_COLS
SCORE_TAIL = N_NODES - TURN_COLS * SCORE_TURNS
SUM_AFTER = {0: 0, 1: 1, 2: 2, 4: 3}
MEET = 6
EXP_TURN = 9
MIX_TURN = 10
assert MIX_TURN + 2 == SCORE_TURNS
assert COUNT_CHUNK * 7 == COLS and COUNT_GROUPS * COUNT_COLS == COUNT_CHUNK
assert EMB_TURNS * EMB_BLOCKS == BLOCKS and EMB_TURNS < TURNS
assert NORM_CHUNKS * NORM_BLOCKS == BLOCKS and NORM_CHUNKS % 2 == 0
assert SCORE_TAIL <= SCORE_COLS and HIGHS * COUNT_COLS <= P and TILE_COLS * P >= TILES


def each_turn(engine, count):
    def run(body):
        body(0)
        with engine.Fori(1, count) as i:
            body(i)
    return run


def held(engine, value):
    return value if isinstance(value, int) else engine.to_reg(value)


def wait_past(engine, semaphore, value):
    if not (isinstance(value, int) and value <= 0):
        engine.wait_ge(semaphore, value)


def bass_graph_session_scores(
    nc, emb, edge_src, edge_dst, edge_val, items, alias, wq_t, bq, wk, bk, wv_t, bv, scores
):
    sorted_edges = nc.dram_tensor("sorted_edges", [P * TILES, RECORD], I32, kind="Internal").ap()
    h1_table = nc.dram_tensor("h1_table", [TABLE_ROWS, DIM], F32, kind="Internal").ap()
    g_table = nc.dram_tensor("g_table", [TABLE_ROWS, DIM], F32, kind="Internal").ap()
    tile_places = nc.dram_tensor("tile_places", [P, TILE_COLS], I32, kind="Internal").ap()
    sorted_v = sorted_edges.rearrange("(p t) w -> p (t w)", p=P)
    emb_v = emb.rearrange("(j p) d -> p j d", p=P)
    h1_v = h1_table.rearrange("(j p) d -> p j d", p=P)
    g_v = g_table.rearrange("(j p) d -> p j d", p=P)

    ctx = ExitStack()
    with ctx:
        def sb(name, shape, dt):
            return ctx.enter_context(nc.sbuf_tensor(name, shape, dt))

        def sem(name):
            return ctx.enter_context(nc.semaphore(name))

        table = sb("table", [P, TABLE_WORDS], F32)
        table_b = table[:, :].rearrange("p (j d) -> p j d", d=DIM)
        work = sb("work", [P, 8192], F32)
        side = sb("side", [P, 4096], F32)

        def in_table(k, dt=F32, cols=COLS):
            return table[:, k * COLS:k * COLS + cols].bitcast(dt)

        src, dst, val = in_table(0, I32), in_table(1, I32), in_table(2)
        dst_ok, near = in_table(3, I32), in_table(4)
        scratch = in_table(5)
        scratch_i = in_table(5, I32)
        halves = table[:, 6 * COLS:7 * COLS].bitcast(BF16)
        high, low = halves[:, 0:COLS], halves[:, COLS:2 * COLS]
        bin_of = table[:, 7 * COLS:8 * COLS + GROUP]
        at = 8 * COLS + GROUP + 1
        is_high = [table[:, at:at + HIGHS * COUNT_CHUNK // 2].bitcast(BF16),
                   work[:, 0:HIGHS * COUNT_CHUNK // 2].bitcast(BF16)]
        at += HIGHS * COUNT_CHUNK // 2
        is_low = [table[:, at:at + LOWS * COUNT_CHUNK // 2].bitcast(BF16),
                  work[:, 4096:4096 + LOWS * COUNT_CHUNK // 2].bitcast(BF16)]
        assert at + LOWS * COUNT_CHUNK // 2 <= TABLE_WORDS
        flat_high, flat_low = is_high, is_low
        is_high = [x.rearrange("p (h c) -> p h c", h=HIGHS) for x in is_high]
        is_low = [x.rearrange("p (l c) -> p l c", l=LOWS) for x in is_low]

        high_i, low_i = side[:, 0:COLS].bitcast(I32), scratch_i

        in_bin = [work[:, k * 256:k * 256 + 222].bitcast(BF16)[:, 0:GROUP * BINS]
                  .rearrange("p (k b) -> p k b", k=GROUP) for k in range(2)]
        ranked = [work[:, 512 + k * 512:512 + k * 512 + GROUP * BINS]
                  .rearrange("p (k b) -> p k b", k=GROUP) for k in range(2)]

        rows = work[:, 0:4096].rearrange("p (s d) -> p s d", d=DIM)
        places = work[:, 4096:8192].rearrange("p (s n) -> p s n", n=BIN_NODES)
        tile_place = side[0:1, 0:P * TILE_COLS].bitcast(I32)

        emb_part = side[:, P * TILE_COLS:P * TILE_COLS + EMB_BLOCKS * DIM].rearrange("p (j d) -> p j d", d=DIM)
        NW = NORM_BLOCKS * DIM
        squares = [side[:, k * NW:(k + 1) * NW].rearrange("p (j d) -> p j d", d=DIM) for k in range(2)]
        normed = [side[:, (2 + k) * NW:(3 + k) * NW].rearrange("p (j d) -> p j d", d=DIM) for k in range(2)]
        row_scale = work[:, (PARTS + 1) * PART * DIM:(PARTS + 1) * PART * DIM + BLOCKS]
        out_stage = [side[:, k * SCORE_COLS:(k + 1) * SCORE_COLS] for k in range(SCORE_SLOTS)]
        sess_sum, part_sum, turned, q_t, select = (
            side[:, TURN_COLS + k * P:TURN_COLS + (k + 1) * P] for k in range(5))

        def seq_part(parity, x):
            at = (parity if x == 0 else x + 1) * PART * DIM
            return work[:, at:at + PART * DIM].rearrange("p (l d) -> p l d", d=DIM)

        patterns = sb("patterns", [P, PART * DIM], F32)
        row_i = patterns[:, 0:256].bitcast(I32)
        row_f = patterns[:, 256:512]
        row_b = patterns[:, 512:592].bitcast(BF16)[:, 0:BINS]
        before, ones_b, zeros_b = (patterns[:, 592 + 64 * k:656 + 64 * k].bitcast(BF16) for k in range(3))
        col8_i = patterns[:, 784:912].bitcast(I32)
        same_col = patterns[:, 912:1040]
        tile_i = patterns[:, 1040:1040 + TILE_COLS].bitcast(I32)
        tile_f = patterns[:, 1080:1080 + TILE_COLS]
        prod = patterns[:, :].rearrange("p (l d) -> p l d", d=DIM)
        part_i = sb("part_i", [P, 1], I32)
        part_f = sb("part_f", [P, 1], F32)
        part_x = sb("part_x", [P, 2], I32)
        part_xf = sb("part_xf", [P, 2], F32)
        ident = sb("ident", [P, P], F32)
        ones_f = sb("ones_f", [P, P], F32)
        col8_f = same_col
        same_high = sb("same_high", [P, HIGHS], F32)
        wq_sb = sb("wq_sb", [DIM, DIM], F32)
        wk_sb = sb("wk_sb", [DIM, DIM + 1], F32)
        wv_sb = sb("wv_sb", [DIM, DIM], F32)
        bq_sb = sb("bq_sb", [DIM, 1], F32)
        bv_sb = sb("bv_sb", [1, DIM], F32)

        spread, counts_masked, bin_tiles, tiles_to, first_tile, base, compared, tile_bin = (
            work[:, 2560 + k * 192:2560 + k * 192 + n]
            for k, n in enumerate((HIGHS * LOWS, LOWS * COUNT_COLS, BINS, BINS, BINS, BINS, BINS, TILE_COLS)))
        bin_tiles_i = compared.bitcast(I32)
        folded_counts = counts_masked[:, 0:LOWS]
        tile_off = sb("tile_off", [P, TILE_COLS], I32)
        pos = [sb(f"pos{q}", [P, QUARTER_COLS], I32) for q in range(4)]
        slot_of = sb("slot_of", [P, QUARTER_COLS], I32)
        tile_of = sb("tile_of", [P, QUARTER_COLS], I32)
        target = [sb(f"target{q}", [P, QUARTER_COLS], I32) for q in range(4)]
        staged = [sb(f"staged{q}", [P, QUARTER_COLS, RECORD], I32) for q in range(4)]
        edges = [sb(f"edges{q}", [P, QUARTER * RECORD], I32) for q in range(4)]
        S = SESSION_GROUPS * LENGTH
        items_f, alias_f, picked, match = (
            work[:, 4096 + k * S:4096 + (k + 1) * S] for k in range(4))
        items_i, alias_i = (work[:, 4096 + k * S:4096 + (k + 1) * S].bitcast(I32) for k in range(4, 6))
        picked_i = sb("picked_i", [P, S + 2 * LENGTH], I32)
        group_items = [sb(f"group_items{k}", [P, LENGTH], I32) for k in range(2)]
        small = TURN_COLS + 5 * P
        spare = (PARTS + 1) * PART * DIM + BLOCKS
        assert spare + P <= 8192
        select_t = [side[:, small:small + P], work[:, spare:spare + P]]
        att, prob = side[:, small + 128:small + 178], side[:, small + 178:small + 228]
        qk = side[:, small + 228:small + 229 + DIM]
        tiny = sb("tiny", [P, 8], F32)

        banks = ctx.enter_context(nc.psum_tensor("banks", [P, 8, 512], F32))
        GB = GROUP * BINS
        counts_ps = banks[0:HIGHS * COUNT_COLS, 0, 0:LOWS * COUNT_COLS]
        all_counts_ps = banks[:, 1, 0:HIGHS * LOWS]
        rank_ps = [banks[:, 2 + k, 0:GB].rearrange("p (k b) -> p k b", k=GROUP) for k in range(2)]
        total_ps = [banks[:, 4 + k, 0:BINS] for k in range(2)]

        def product_ps(q, k):
            return banks[:, 4 * (q % 2) + k // 2, 256 * (k % 2):256 * (k % 2) + 256]

        def pair(k):
            return banks[:, 2 * k:2 * k + 2, :].rearrange("p b n -> p (b n)")

        sess_t_ps, q_ps, qk_ps = banks[:, 6, 0:128], banks[:, 6, 128:256], banks[:, 6, 256:385]
        mix_ps, emb_ps, select_ps = banks[:, 7, 0:128], banks[:, 7, 128:256], banks[:, 7, 256:384]

        dst_loaded = sem("dst_loaded")
        edges_loaded = sem("edges_loaded")
        items_loaded = sem("items_loaded")
        weights_loaded = sem("weights_loaded")
        patterns_made = sem("patterns_made")
        constants_made = sem("constants_made")
        dve_step = sem("dve_step")
        highs_lows_made = sem("highs_lows_made")
        counted = sem("counted")
        counts_done = sem("counts_done")
        spread_made = sem("spread_made")
        counts_spread = sem("counts_spread")
        edges_split = sem("edges_split")
        in_bin_made = sem("in_bin_made")
        ranked_by_pe = sem("ranked_by_pe")
        rank_taken = sem("rank_taken")
        rank_step = sem("rank_step")
        base_moved = sem("base_moved")
        target_ready = [sem(f"target_ready{q}") for q in range(4)]
        staged_ready = [sem(f"staged_ready{q}") for q in range(4)]
        scattered = [sem(f"scattered{q}") for q in range(4)]
        places_computed = sem("places_computed")
        places_saved = sem("places_saved")
        places_back = sem("places_back")
        edges_in = [[sem(f"edges_in{y}{q}") for q in range(4)] for y in range(LAYERS)]
        gathered = [[sem(f"gathered{y}{q}") for q in range(4)] for y in range(LAYERS)]
        weights_made = [[sem(f"weights_made{y}{q}") for q in range(4)] for y in range(LAYERS)]
        products = [[sem(f"products{y}{q}") for q in range(4)] for y in range(LAYERS)]
        folded = [[sem(f"folded{y}{q}") for q in range(4)] for y in range(LAYERS)]
        folds = [sem(f"folds{y}") for y in range(LAYERS)]
        h1_written = sem("h1_written")
        items_picked = sem("items_picked")
        pick_step = sem("pick_step")
        emb_in = sem("emb_in")
        emb_added = sem("emb_added")
        g_written = sem("g_written")
        squared = [sem(f"squared{k}") for k in range(2)]
        summed = [sem(f"summed{k}") for k in range(2)]
        rooted = sem("rooted")
        norm_step = sem("norm_step")
        normalized = [sem(f"normalized{k}") for k in range(2)]
        g_turned = [sem(f"g_turned{k}") for k in range(2)]
        g_placed = [sem(f"g_placed{k}") for k in range(2)]
        numbers_split = sem("numbers_split")
        numbers_turned = sem("numbers_turned")
        edges_masked = sem("edges_masked")
        pool_step = sem("pool_step")
        indices_ready = sem("indices_ready")
        head_in = [sem(f"head_in{k}") for k in range(2)]
        body_in = [sem(f"body_in{k}") for k in range(PARTS - 1)]
        att_step = sem("att_step")
        sess_summed = sem("sess_summed")
        sess_turned = sem("sess_turned")
        sess_placed = sem("sess_placed")
        q_made = sem("q_made")
        q_biased = sem("q_biased")
        qk_made = sem("qk_made")
        att_made = sem("att_made")
        exp_made = sem("exp_made")
        seq_weighted = sem("seq_weighted")
        seq_mixed = sem("seq_mixed")
        mix_placed = sem("mix_placed")
        emb_made = sem("emb_made")
        emb_squared = sem("emb_squared")
        emb_rooted = sem("emb_rooted")
        selected = sem("selected")
        select_turned = sem("select_turned")
        select_placed = sem("select_placed")
        scored = [sem(f"scored{k}") for k in range(SCORE_SLOTS)]
        taken = [sem(f"taken{k}") for k in range(SCORE_SLOTS)]
        stored = [sem(f"stored{k}") for k in range(SCORE_SLOTS)]

        def uses_before(k, g, i):
            return g * (SCORE_TURNS + (k == 0)) + i

        def all_groups(engine, scores_of):
            @each_turn(engine, (SESSION_GROUPS - 2) // 2)
            def _(i):
                for parity in range(2):
                    scores_of(i * 2 + parity, parity, True)
            scores_of(SESSION_GROUPS - 2, 0, True)
            scores_of(SESSION_GROUPS - 1, 1, False)

        block = ctx.enter_context(nc.Block())

        @block.sync
        def _(sp):
            sp.dma_start(dst, edge_dst).then_inc(dst_loaded, 16)
            sp.dma_start(src, edge_src).then_inc(edges_loaded, 16)
            sp.dma_start(val, edge_val).then_inc(edges_loaded, 16)
            sp.dma_start(wq_sb[:, :], wq_t).then_inc(weights_loaded, 16)
            sp.dma_start(wk_sb[:, 0:DIM], wk).then_inc(weights_loaded, 16)
            sp.dma_start(wk_sb[:, DIM:DIM + 1], bk).then_inc(weights_loaded, 16)
            sp.dma_start(wv_sb[:, :], wv_t).then_inc(weights_loaded, 16)
            sp.dma_start(bq_sb[:, :], bq).then_inc(weights_loaded, 16)
            sp.dma_start(bv_sb[:, :], bv).then_inc(weights_loaded, 16)
            sp.wait_ge(constants_made, 1)
            for k in range(5):
                width = TILES * RECORD // 5
                sp.dma_start(sorted_v[:, k * width:(k + 1) * width],
                             work[:, 0:width].bitcast(I32)).then_inc(h1_written, 16)

            sp.wait_ge(places_computed, 1)
            sp.dma_start(tile_places, tile_off[:, :]).then_inc(places_saved, 16)
            sp.wait_ge(places_saved, 16)
            sp.dma_start(tile_place, tile_places.rearrange("p c -> (p c)")[None, :]).then_inc(places_back, 16)

            for q in range(4):
                sp.wait_ge(scattered[q], 16 * QUARTER_COLS * SORT_TURNS)

            def load_edges(y, i):
                rows_before = held(sp, i * (16 * QUARTER))
                for q in range(4):
                    sp.wait_ge(scattered[3], 16 * QUARTER_COLS * SORT_TURNS)
                    wait_past(sp, gathered[y][q], rows_before)
                    wait_past(sp, weights_made[y][q], i)
                    sp.dma_start(edges[q][:, :], sorted_v[:, bass.ds(
                        i * (BODY_TILES * RECORD) + q * QUARTER * RECORD, QUARTER * RECORD)]
                    ).then_inc(edges_in[y][q], 16)

            @each_turn(sp, TURNS)
            def _(i):
                load_edges(0, i)

            for q in range(4):
                sp.wait_ge(products[0][q], TURNS)
            sp.dma_start(items_i.rearrange("p (g l) -> p g l", l=LENGTH),
                         items.rearrange("(g p) l -> p g l", p=P)).then_inc(items_loaded, 16)
            sp.dma_start(alias_i.rearrange("p (g l) -> p g l", l=LENGTH),
                         alias.rearrange("(g p) l -> p g l", p=P)).then_inc(items_loaded, 16)
            sp.wait_ge(folded[0][3], TURNS)
            sp.dma_start(h1_v, table_b).then_inc(h1_written, 16)
            sp.wait_ge(gathered[0][3], 16 * QUARTER * TURNS)

            @each_turn(sp, EMB_TURNS)
            def _(i):
                load_edges(1, i)
                wait_past(sp, emb_added, i)
                sp.dma_start(emb_part, emb_v[:, bass.ds(i * EMB_BLOCKS, EMB_BLOCKS), :]).then_inc(emb_in, 16)

            with sp.Fori(EMB_TURNS, TURNS) as i:
                load_edges(1, i)

            sp.wait_ge(folded[1][3], TURNS)
            sp.dma_start(g_v, table_b).then_inc(g_written, 16)

            @each_turn(sp, SESSION_GROUPS)
            def _(g):
                @each_turn(sp, SCORE_TURNS)
                def _(i):
                    for k in range(SCORE_SLOTS):
                        sp.wait_ge(taken[k], uses_before(k, g, i) + 1)
                        sp.dma_start(scores[bass.ds(g * P, P), bass.ds(i * TURN_COLS + k * SCORE_COLS, SCORE_COLS)],
                                     out_stage[k]).then_inc(stored[k], 16)
                sp.wait_ge(taken[0], uses_before(0, g, SCORE_TURNS) + 1)
                sp.dma_start(scores[bass.ds(g * P, P), TURN_COLS * SCORE_TURNS:N_NODES],
                             out_stage[0][:, 0:SCORE_TAIL]).then_inc(stored[0], 16)
            for k in range(SCORE_SLOTS):
                sp.wait_ge(stored[k], 16 * uses_before(k, SESSION_GROUPS, 0))

        @block.gpsimd
        def _(pool):
            pool.iota(row_i, [[1, BIN_NODES]], base=0, channel_multiplier=0).then_inc(patterns_made, 1)
            pool.iota(part_i[:, :], [[0, 1]], base=0, channel_multiplier=1).then_inc(patterns_made, 1)
            pool.iota(tile_i, [[1, TILE_COLS]], base=0, channel_multiplier=TILE_COLS).then_inc(patterns_made, 1)
            pool.iota(col8_i, [[0, LOWS], [1, COUNT_COLS]], base=0, channel_multiplier=0).then_inc(patterns_made, 1)

            pool.wait_ge(edges_loaded, 32)
            fixed = side[:, 0:COLS].bitcast(I32)
            pool.wait_ge(numbers_turned, 1)
            pool.tensor_scalar(fixed, src, 0.0, float(N_NODES), ALU.is_lt, ALU.mult).then_inc(pool_step, 1)
            pool.wait_ge(pool_step, 1)
            pool.tensor_tensor(src, src, fixed, ALU.add).then_inc(pool_step, 1)
            pool.wait_ge(pool_step, 2)
            pool.tensor_scalar(src, src, 0.0, float(N_NODES - 1), ALU.max, ALU.min).then_inc(edges_masked, 1)

            @each_turn(pool, SORT_TURNS)
            def _(i):
                turn = held(pool, i + 1)
                for q in range(4):
                    pool.wait_ge(h1_written, 16 * 5)
                    pool.wait_ge(target_ready[q], turn)
                    pool.wait_ge(staged_ready[q], turn)
                    for c in range(QUARTER_COLS):
                        pool.indirect_dma_start(
                            sorted_edges, bass.IndirectOffsetOnAxis(target[q][:, c:c + 1], 0),
                            staged[q][:, c, :], None,
                        ).then_inc(scattered[q], 16)

            def gather_rows(y, source):
                @each_turn(pool, TURNS)
                def _(i):
                    edges_so_far = held(pool, (i + 1) * 16)
                    for q in range(4):
                        pool.wait_ge(h1_written, 16 * (5 + y))
                        pool.wait_ge(edges_in[y][q], edges_so_far)
                        wait_past(pool, products[y][q], i)
                        for t in range(QUARTER):
                            pool.indirect_dma_start(
                                rows[:, q * QUARTER + t, :], None, source,
                                bass.IndirectOffsetOnAxis(edges[q][:, t * RECORD:t * RECORD + 1], 0),
                            ).then_inc(gathered[y][q], 16)

            gather_rows(0, emb)
            gather_rows(1, h1_table)

            @each_turn(pool, SESSION_GROUPS // 2)
            def _(i):
                for parity in range(2):
                    g = i * 2 + parity
                    groups = held(pool, g + 1)
                    mixed = [held(pool, g * PARTS - PARTS + (x + 1 if x else 0)) for x in range(PARTS)]
                    for x in range(PARTS):
                        pool.wait_ge(g_written, 16)
                        pool.wait_ge(indices_ready, groups)
                        wait_past(pool, seq_mixed, mixed[x])
                        for l in range(PART):
                            pool.indirect_dma_start(
                                seq_part(parity, x)[:, l, :], None, g_table,
                                bass.IndirectOffsetOnAxis(group_items[parity][:, x * PART + l:x * PART + l + 1], 0),
                            ).then_inc(body_in[x - 1] if x else head_in[parity], 16)

        @block.tensor
        def _(pe):
            pe.wait_ge(constants_made, 3)
            HC, LC = HIGHS * COUNT_COLS, LOWS * COUNT_COLS
            pe.matmul(counts_ps, zeros_b[:, 0:HC], zeros_b[:, 0:LC], start=True, stop=False, skip_group_check=True)

            def count(k, uses):
                wait_past(pe, highs_lows_made, uses)
                for c in range(COUNT_GROUPS):
                    last = pe.matmul(counts_ps, flat_high[k][:, c::COUNT_GROUPS], flat_low[k][:, c::COUNT_GROUPS],
                                     start=False, stop=False, skip_group_check=True)
                last.then_inc(counted, 1)

            @each_turn(pe, 3)
            def _(i):
                count(0, i * 2 + 1)
                count(1, i * 2 + 2)
            count(0, 7)
            pe.matmul(counts_ps, zeros_b[:, 0:HC], zeros_b[:, 0:LC], start=False, stop=True,
                      skip_group_check=True).then_inc(counts_done, 1)
            pe.wait_ge(spread_made, 1)
            pe.matmul(all_counts_ps, ones_f[0:HC, :], spread[0:HC, :], start=True, stop=True).then_inc(counts_spread, 1)

            @each_turn(pe, SORT_TURNS)
            def _(i):
                for c in range(8):
                    k = c % 2
                    pe.wait_ge(in_bin_made, i * 8 + c + 1)
                    wait_past(pe, rank_taken, i * 8 + c - 1)
                    o = in_bin[k]
                    pe.matmul(rank_ps[k], before, o, start=True, stop=False, skip_group_check=True)
                    pe.matmul(rank_ps[k][:, 1:3, :], ones_b,
                              o[:, 0:1, :].to_broadcast([P, 2, BINS]), start=False, stop=False, skip_group_check=True)
                    pe.matmul(rank_ps[k][:, 2:3, :], ones_b, o[:, 1:2, :], start=False, stop=True, skip_group_check=True)
                    for x in range(GROUP):
                        last = pe.matmul(total_ps[k], ones_b, o[:, x, :], start=(x == 0), stop=(x == GROUP - 1))
                    last.then_inc(ranked_by_pe, 1)

            def layer(y):
                @each_turn(pe, TURNS)
                def _(i):
                    for q in range(4):
                        pe.wait_ge(gathered[y][q], (i + 1) * (16 * QUARTER))
                        pe.wait_ge(weights_made[y][q], i + 1)
                        wait_past(pe, folded[y][(q + 2) % 4], i + (q >= 2))
                        for t in range(QUARTER):
                            for h in range(2):
                                last = pe.matmul(
                                    product_ps(q, t)[:, h * DIM:(h + 1) * DIM],
                                    places[:, (q % 2) * QUARTER + t, h * P:(h + 1) * P],
                                    rows[:, q * QUARTER + t, :], start=True, stop=True)
                        last.then_inc(products[y][q], 1)

            layer(0)
            layer(1)

            pe.wait_ge(folded[1][3], TURNS)
            @each_turn(pe, NORM_CHUNKS // 2)
            def _(i):
                for k in range(2):
                    pe.wait_ge(normalized[k], i + 1)
                    wait_past(pe, g_placed[k], i)
                    for j in range(NORM_BLOCKS):
                        last = pe.transpose(banks[:, 2 * k + j // 4, (j % 4) * P:(j % 4 + 1) * P],
                                            normed[k][:, j, :], ident[:, :])
                    last.then_inc(g_turned[k], 1)

            pe.wait_ge(weights_loaded, 16 * 6)
            for k in range(2):
                pe.wait_ge(g_placed[k], NORM_CHUNKS // 2)

            def turn_sum(g):
                pe.wait_ge(sess_summed, g + 1)
                pe.transpose(sess_t_ps, sess_sum, ident[:, :]).then_inc(sess_turned, 1)

            def make_q(g):
                pe.wait_ge(sess_placed, g + 1)
                pe.matmul(q_ps, wq_sb[:, :], turned, start=True, stop=True).then_inc(q_made, 1)

            def make_qk(g):
                pe.wait_ge(q_biased, g + 1)
                pe.matmul(qk_ps, q_t, wk_sb[:, :], start=True, stop=True).then_inc(qk_made, 1)

            def mix(g, parity, parts):
                for x in parts:
                    pe.wait_ge(seq_weighted, g * PARTS + x + 1)
                    for l in range(PART // 2):
                        last = pe.matmul(mix_ps, seq_part(parity, x)[:, l, :], ident[:, :], start=(x == 0 and l == 0),
                                         stop=(x == PARTS - 1 and l == PART // 2 - 1))
                    last.then_inc(seq_mixed, 1)

            def make_emb(g):
                pe.wait_ge(mix_placed, g + 1)
                pe.matmul(emb_ps, turned, wv_sb[:, :], start=True, stop=False)
                pe.matmul(emb_ps, ones_f[0:1, :], bv_sb[:, :], start=False, stop=True).then_inc(emb_made, 1)

            def turn_select(g):
                pe.wait_ge(selected, g + 1)
                pe.transpose(select_ps, select, ident[:, :]).then_inc(select_turned, 1)

            def score(k, g, parity, i, col, width):
                wait_past(pe, taken[k], uses_before(k, g, i))
                for h in range(-(-width // 512)):
                    w = min(512, width - 512 * h)
                    last = pe.matmul(banks[:, 2 * k + h, 0:w], select_t[parity],
                                     table[:, bass.ds(col + 512 * h, w)], start=True, stop=True)
                last.then_inc(scored[k], 1)

            def slot(k, g, parity, i):
                score(k, g, parity, i, i * TURN_COLS + k * SCORE_COLS, SCORE_COLS)

            def scores_of(g, parity, more):
                pe.wait_ge(select_placed, g + 1)
                @each_turn(pe, MEET)
                def _(i):
                    for k in range(SCORE_SLOTS):
                        slot(k, g, parity, i)
                slot(0, g, parity, MEET)
                if more:
                    turn_sum(g + 1)
                slot(1, g, parity, MEET)
                if more:
                    make_q(g + 1)
                slot(2, g, parity, MEET)
                if more:
                    make_qk(g + 1)
                with pe.Fori(MEET + 1, MIX_TURN) as i:
                    for k in range(SCORE_SLOTS):
                        slot(k, g, parity, i)
                for k in range(SCORE_SLOTS):
                    slot(k, g, parity, MIX_TURN)
                    if more:
                        mix(g + 1, 1 - parity, range(2 * k, min(2 * k + 2, PARTS)))
                slot(0, g, parity, MIX_TURN + 1)
                if more:
                    make_emb(g + 1)
                slot(1, g, parity, MIX_TURN + 1)
                slot(2, g, parity, MIX_TURN + 1)
                if more:
                    turn_select(g + 1)
                score(0, g, parity, SCORE_TURNS, TURN_COLS * SCORE_TURNS, SCORE_TAIL)

            turn_sum(0)
            make_q(0)
            make_qk(0)
            mix(0, 0, range(PARTS))
            make_emb(0)
            turn_select(0)
            all_groups(pe, scores_of)

        @block.scalar
        def _(act):
            act.wait_ge(numbers_split, 1)
            act.copy(high, high_i).then_inc(numbers_turned, 1)
            act.wait_ge(numbers_split, 2)
            act.copy(low, low_i).then_inc(numbers_turned, 1)
            act.wait_ge(numbers_split, 3)
            act.copy(bin_of[:, 0:COLS], bin_of[:, 0:COLS].bitcast(I32)).then_inc(numbers_turned, 1)
            act.wait_ge(numbers_split, 4)
            act.copy(near, near.bitcast(I32)).then_inc(numbers_turned, 1)
            act.wait_ge(numbers_turned, 4)

            act.wait_ge(edges_split, 1)
            act.wait_ge(edges_masked, 1)
            @each_turn(act, SORT_TURNS)
            def _(i):
                for q in range(4):
                    wait_past(act, scattered[q], i * (16 * QUARTER_COLS))
                    cols = bass.ds(i * BODY_COLS + q * QUARTER_COLS, QUARTER_COLS)
                    act.copy(staged[q][:, :, 0], src[:, cols])
                    act.copy(staged[q][:, :, 1].bitcast(F32), near[:, cols])
                    act.copy(staged[q][:, :, 2].bitcast(F32), val[:, cols]).then_inc(staged_ready[q], 1)

            def group_indices(g, k):
                act.copy(group_items[k][:, :], picked_i[:, bass.ds(g * LENGTH, LENGTH)]).then_inc(indices_ready, 1)

            act.wait_ge(items_picked, 2)
            group_indices(0, 0)
            group_indices(1, 1)

            act.wait_ge(folded[1][3], TURNS)

            @each_turn(act, NORM_CHUNKS // 2)
            def _(i):
                for k in range(2):
                    wait_past(act, summed[k], i)
                    blocks = bass.ds(i * (2 * NORM_BLOCKS) + k * NORM_BLOCKS, NORM_BLOCKS)
                    act.activation(squares[k], table_b[:, blocks, :], ACT.Square).then_inc(squared[k], 1)
            for k in range(2):
                act.wait_ge(summed[k], NORM_CHUNKS // 2)
            act.activation(row_scale, row_scale, ACT.Sqrt).then_inc(rooted, 1)

            act.wait_ge(g_written, 16)

            @each_turn(act, NORM_CHUNKS // 2)
            def _(i):
                for k in range(2):
                    act.wait_ge(g_turned[k], i + 1)
                    at = i * (2 * NORM_BLOCKS * P) + k * NORM_BLOCKS * P
                    act.copy(table[:, bass.ds(at, NW)], pair(k)[:, 0:NW]).then_inc(g_placed[k], 1)

            def bias_q(g):
                act.wait_ge(q_made, g + 1)
                act.activation(q_t, q_ps, ACT.Identity, bias=bq_sb[:, :]).then_inc(q_biased, 1)

            def exponentials(g, parity):
                act.wait_ge(att_made, g + 1)
                act.activation(prob, att, ACT.Exp, bias=tiny[:, 0:1], scale=float(DIM) ** -0.5,
                               accum_out=tiny[:, 1:2]).then_inc(exp_made, 1)
                group_indices(g + 2, parity)

            def emb_norms(g):
                act.wait_ge(emb_made, g + 1)
                act.activation(q_t, emb_ps, ACT.Square, accum_out=tiny[:, 3:4]).then_inc(emb_squared, 1)
                act.wait_ge(emb_squared, g + 1)
                act.activation(tiny[:, 4:5], tiny[:, 3:4], ACT.Sqrt).then_inc(emb_rooted, 1)

            def take(k, g, i, width):
                act.wait_ge(scored[k], uses_before(k, g, i) + 1)
                wait_past(act, stored[k], uses_before(k, g, i) * 16)
                act.copy(out_stage[k][:, 0:width], pair(k)[:, 0:width]).then_inc(taken[k], 1)

            def scores_of(g, parity, more):
                @each_turn(act, MEET)
                def _(i):
                    take(0, g, i, SCORE_COLS)
                    take(2, g, i, SCORE_COLS)
                take(0, g, MEET, SCORE_COLS)
                if more:
                    bias_q(g + 1)
                take(1, g, MEET, SCORE_COLS)
                take(2, g, MEET, SCORE_COLS)
                with act.Fori(MEET + 1, EXP_TURN) as i:
                    for k in range(SCORE_SLOTS):
                        take(k, g, i, SCORE_COLS)
                if more:
                    exponentials(g + 1, 1 - parity)
                for i in range(EXP_TURN, SCORE_TURNS):
                    for k in range(SCORE_SLOTS):
                        take(k, g, i, SCORE_COLS)
                        if more and i == MIX_TURN + 1 and k == 0:
                            emb_norms(g + 1)
                take(0, g, SCORE_TURNS, SCORE_TAIL)

            bias_q(0)
            exponentials(0, 0)
            emb_norms(0)
            all_groups(act, scores_of)

        @block.vector
        def _(dve):
            steps = [0]

            def done(instruction):
                steps[0] += 1
                instruction.then_inc(dve_step, 1)
                dve.wait_ge(dve_step, steps[0])

            dve.memset(work[:, :], 0.0).then_inc(constants_made, 1)
            dve.memset(ones_b, 1.0).then_inc(constants_made, 1)
            dve.memset(zeros_b, 0.0).then_inc(constants_made, 1)
            done(dve.memset(ones_f[:, :], 1.0))
            done(dve.memset(bin_of[:, COLS:COLS + GROUP], 0.0))
            for q in range(4):
                done(dve.memset(staged[q][:, :, :], 0))
            dve.wait_ge(patterns_made, 4)
            done(dve.tensor_copy(row_f, row_i))
            done(dve.tensor_copy(part_f[:, :], part_i[:, :]))
            done(dve.tensor_copy(tile_f, tile_i))
            done(dve.tensor_copy(row_b, row_f[:, 0:BINS]))
            done(dve.tensor_scalar(ident[:, :], row_f[:, 0:P], part_f[:, 0:1], None, ALU.is_equal))
            done(dve.tensor_scalar(before, row_f[:, 0:P], part_f[:, 0:1], None, ALU.is_gt))
            done(dve.tensor_scalar(part_x[:, 0:1], part_i[:, :], COUNT_COLS - 1, None, ALU.bitwise_and))
            done(dve.tensor_scalar(part_x[:, 1:2], part_i[:, :], 3, None, ALU.logical_shift_right))
            done(dve.tensor_copy(part_xf[:, :], part_x[:, :]))
            done(dve.tensor_copy(col8_f, col8_i))
            done(dve.tensor_scalar(same_col, col8_f, part_xf[:, 0:1], None, ALU.is_equal))
            done(dve.tensor_scalar(same_high[:, :], row_f[:, 0:HIGHS], part_xf[:, 1:2], None, ALU.is_equal))

            dve.wait_ge(dst_loaded, 16)
            done(dve.tensor_scalar(dst_ok, dst, 0.0, float(N_NODES - 1), ALU.max, ALU.min))
            near_i = near.bitcast(I32)
            dve.tensor_scalar(high_i, dst_ok, 12, None, ALU.logical_shift_right).then_inc(numbers_split, 1)
            dve.tensor_scalar(low_i, dst_ok, 8, LOWS - 1, ALU.logical_shift_right,
                              ALU.bitwise_and).then_inc(numbers_split, 1)
            dve.tensor_scalar(bin_of[:, 0:COLS].bitcast(I32), dst_ok, 8, None,
                              ALU.logical_shift_right).then_inc(numbers_split, 1)
            dve.tensor_scalar(near_i, dst_ok, BIN_NODES - 1, None, ALU.bitwise_and).then_inc(numbers_split, 1)

            def highs_lows(k, col):
                for h in range(HIGHS):
                    dve.tensor_scalar(is_high[k][:, h, :], high[:, bass.ds(col, COUNT_CHUNK)], float(h), None,
                                      ALU.is_equal)
                for l in range(LOWS):
                    last = dve.tensor_scalar(is_low[k][:, l, :], low[:, bass.ds(col, COUNT_CHUNK)], float(l), None,
                                             ALU.is_equal)
                last.then_inc(highs_lows_made, 1)

            dve.wait_ge(numbers_turned, 2)
            highs_lows(0, 0)
            dve.wait_ge(h1_written, 16 * 5)
            @each_turn(dve, 3)
            def _(i):
                wait_past(dve, counted, i * 2)
                highs_lows(1, i * (2 * COUNT_CHUNK) + COUNT_CHUNK)
                dve.wait_ge(counted, i * 2 + 1)
                highs_lows(0, i * (2 * COUNT_CHUNK) + 2 * COUNT_CHUNK)

            dve.wait_ge(edges_loaded, 32)
            done(dve.tensor_tensor(scratch, dst_ok, dst, ALU.is_equal))
            dve.tensor_tensor(val, val, scratch, ALU.mult).then_inc(edges_split, 1)
            dve.wait_ge(edges_split, 1)

            dve.wait_ge(counts_done, 1)
            HC = HIGHS * COUNT_COLS
            done(dve.tensor_tensor(scratch[0:HC, 0:LOWS * COUNT_COLS], counts_ps, same_col[0:HC, :], ALU.mult))
            done(dve.tensor_reduce(folded_counts[0:HC, :], scratch[0:HC, 0:LOWS * COUNT_COLS].rearrange(
                "p (l c) -> p l c", l=LOWS), AX.X, ALU.add))
            dve.tensor_tensor(spread[0:HC, :].rearrange("p (h l) -> p h l", h=HIGHS),
                              same_high[0:HC, :, None].to_broadcast([HC, HIGHS, LOWS]),
                              folded_counts[0:HC, None, :].to_broadcast([HC, HIGHS, LOWS]),
                              ALU.mult).then_inc(spread_made, 1)
            dve.wait_ge(counts_spread, 1)
            done(dve.tensor_scalar(bin_tiles_i, all_counts_ps[:, 0:BINS], float(P - 1), None, ALU.add))
            done(dve.tensor_scalar(bin_tiles_i, bin_tiles_i, 7, None, ALU.logical_shift_right))
            done(dve.tensor_copy(bin_tiles, bin_tiles_i))
            done(dve.tensor_tensor_scan(tiles_to, ones_f[:, 0:1].to_broadcast([P, BINS]), bin_tiles,
                                        0.0, ALU.mult, ALU.add))
            done(dve.tensor_tensor(first_tile, tiles_to, bin_tiles, ALU.subtract))
            done(dve.tensor_scalar(base, first_tile, float(P), None, ALU.mult))

            def one_hot(k, col):
                for x in range(GROUP):
                    last = dve.tensor_scalar(in_bin[k][:, x, :], row_b, bin_of[:, bass.ds(col + x, 1)], None,
                                             ALU.is_equal)
                last.then_inc(in_bin_made, 1)

            dve.wait_ge(numbers_turned, 3)
            one_hot(0, 0)
            @each_turn(dve, SORT_TURNS)
            def _(i):
                for c in range(8):
                    k, q = c % 2, c // 2
                    one_hot(1 - k, i * BODY_COLS + (c + 1) * GROUP)
                    dve.wait_ge(ranked_by_pe, i * 8 + c + 1)
                    wait_past(dve, base_moved, i * 8 + c)
                    dve.tensor_tensor(ranked[k], rank_ps[k], base[:, None, :].to_broadcast([P, GROUP, BINS]),
                                      ALU.add).then_inc(rank_step, 1)
                    dve.wait_ge(rank_step, (i * 8 + c) * 2 + 1)
                    dve.tensor_tensor(base, base, total_ps[k], ALU.add).then_inc(base_moved, 1)
                    dve.tensor_tensor(ranked[k], ranked[k], in_bin[k], ALU.mult).then_inc(rank_step, 1)
                    dve.wait_ge(rank_step, (i * 8 + c) * 2 + 2)
                    with nc.allow_low_precision(reason="positions are whole numbers below 2**24"):
                        dve.tensor_reduce(pos[q][:, k * GROUP:(k + 1) * GROUP], ranked[k], AX.X,
                                          ALU.add).then_inc(rank_taken, 1)
                    if k == 1:
                        dve.wait_ge(rank_taken, i * 8 + c + 1)
                        dve.tensor_scalar(slot_of[:, :], pos[q][:, :], P - 1, None, ALU.bitwise_and).then_inc(pick_step, 1)
                        dve.tensor_scalar(tile_of[:, :], pos[q][:, :], 7, None, ALU.logical_shift_right).then_inc(pick_step, 1)
                        dve.wait_ge(pick_step, (i * 4 + q) * 2 + 2)
                        wait_past(dve, scattered[q], i * (16 * QUARTER_COLS))
                        dve.scalar_tensor_tensor(out=target[q][:, :], in0=slot_of[:, :], scalar=float(TILES),
                                                 in1=tile_of[:, :], op0=ALU.mult, op1=ALU.add).then_inc(target_ready[q], 1)

            for c in range(TILE_COLS):
                done(dve.tensor_scalar(compared, first_tile, tile_f[:, c:c + 1], None, ALU.is_le, ALU.add,
                                       accum_out=tile_bin[:, c:c + 1]))
            dve.tensor_scalar(tile_off[:, :], tile_bin[:, :], -1.0, float(2 * DIM), ALU.add,
                              ALU.mult).then_inc(places_computed, 1)

            for q in range(4):
                dve.wait_ge(staged_ready[q], SORT_TURNS)
            done(dve.memset(table[:, :], 0.0))
            dve.wait_ge(places_back, 16)

            def weights(q, t):
                e = edges[q][:, t * RECORD:(t + 1) * RECORD].bitcast(F32)
                return dve.tensor_scalar(places[:, (q % 2) * QUARTER + t, :], row_f, e[:, 1:2], e[:, 2:3],
                                         ALU.is_equal, ALU.mult)

            def layer(y):
                def fold(i, q, ahead):
                    dve.wait_ge(products[y][q], i + 1)
                    q2 = (q + 2) % 4
                    if ahead:
                        dve.wait_ge(edges_in[y][q2], (i + 1 + (q >= 2)) * 16)
                    _, off = nc.values_load_multi_w_load_instructions(
                        tile_place[0:1, bass.ds(i * BODY_TILES + q * QUARTER, QUARTER)], engines=[dve.engine],
                        min_val=0, max_val=TABLE_WORDS - BIN_NODES,
                        skip_runtime_bounds_check_because="the places are computed on the chip, one of BINS")
                    for t in range(QUARTER):
                        into = table[:, bass.ds(off[t], 2 * DIM)]
                        if t:
                            wait_past(dve, folds[y], (i * 4 + q) * (QUARTER - 1) + t)
                        else:
                            wait_past(dve, folded[y][(q + 3) % 4], i + (q > 0))
                        dve.tensor_tensor(into, into, product_ps(q, t), ALU.add).then_inc(
                            folds[y] if t < QUARTER - 1 else folded[y][q], 1)
                        if ahead:
                            made = weights(q2, t)
                    if ahead:
                        made.then_inc(weights_made[y][q2], 1)

                for q in range(2):
                    dve.wait_ge(edges_in[y][q], 16)
                    for t in range(QUARTER):
                        made = weights(q, t)
                    made.then_inc(weights_made[y][q], 1)
                @each_turn(dve, TURNS - 1 if y == 0 else EMB_TURNS)
                def _(i):
                    for q in range(4):
                        fold(i, q, True)
                    if y:
                        dve.wait_ge(emb_in, (i + 1) * 16)
                        dve.wait_ge(folded[y][3], i + 1)
                        part = table_b[:, bass.ds(i * EMB_BLOCKS, EMB_BLOCKS), :]
                        dve.tensor_tensor(part, part, emb_part, ALU.add).then_inc(emb_added, 1)
                        dve.wait_ge(emb_added, i + 1)
                if y:
                    with dve.Fori(EMB_TURNS, TURNS - 1) as i:
                        for q in range(4):
                            fold(i, q, True)
                for q in range(4):
                    fold(TURNS - 1, q, q < 2)

            layer(0)

            dve.wait_ge(items_loaded, 32)
            dve.wait_ge(gathered[0][3], 16 * QUARTER * TURNS)
            for x, n, y in ((items_i, N_NODES, items_f), (alias_i, LENGTH, alias_f)):
                done(dve.tensor_scalar(y, x, 0.0, float(n), ALU.is_lt, ALU.mult))
                done(dve.tensor_tensor(y, y, x, ALU.add))
            done(dve.tensor_scalar(items_f, items_f, 0.0, float(N_NODES - 1), ALU.max, ALU.min))
            done(dve.memset(picked, 0.0))
            items_g = items_f.rearrange("p (g l) -> p g l", l=LENGTH)
            alias_g = alias_f.rearrange("p (g l) -> p g l", l=LENGTH)
            match_g = match.rearrange("p (g l) -> p g l", l=LENGTH)
            picks = SORT_TURNS * 8
            @each_turn(dve, LENGTH)
            def _(j):
                dve.wait_ge(pick_step, j * 2 + picks)
                dve.scalar_tensor_tensor(
                    out=match_g, in0=alias_g, scalar=row_f[:, bass.ds(j, 1)],
                    in1=items_g[:, :, bass.ds(j, 1)].to_broadcast([P, SESSION_GROUPS, LENGTH]),
                    op0=ALU.is_equal, op1=ALU.mult).then_inc(pick_step, 1)
                dve.wait_ge(pick_step, j * 2 + picks + 1)
                dve.tensor_tensor(picked, picked, match, ALU.add).then_inc(pick_step, 1)
            dve.wait_ge(pick_step, picks + 2 * LENGTH)
            dve.memset(picked_i[:, S:S + 2 * LENGTH], 0).then_inc(items_picked, 1)
            dve.tensor_copy(picked_i[:, 0:S], picked).then_inc(items_picked, 1)

            dve.wait_ge(h1_written, 16 * 6)
            dve.wait_ge(items_picked, 2)
            layer(1)

            @each_turn(dve, NORM_CHUNKS // 2)
            def _(i):
                for k in range(2):
                    dve.wait_ge(squared[k], i + 1)
                    dve.tensor_reduce(row_scale[:, bass.ds(i * (2 * NORM_BLOCKS) + k * NORM_BLOCKS, NORM_BLOCKS)],
                                      squares[k], AX.X, ALU.add).then_inc(summed[k], 1)
            dve.wait_ge(rooted, 1)
            dve.tensor_scalar(row_scale, row_scale, EPS * (LAYERS + 1), None, ALU.max).then_inc(norm_step, 1)
            dve.wait_ge(norm_step, 1)
            dve.reciprocal(row_scale, row_scale).then_inc(norm_step, 1)
            dve.wait_ge(norm_step, 2)

            @each_turn(dve, NORM_CHUNKS // 2)
            def _(i):
                for k in range(2):
                    wait_past(dve, g_turned[k], i)
                    blocks = bass.ds(i * (2 * NORM_BLOCKS) + k * NORM_BLOCKS, NORM_BLOCKS)
                    dve.tensor_tensor(normed[k], table_b[:, blocks, :],
                                      row_scale[:, blocks][:, :, None].to_broadcast([P, NORM_BLOCKS, DIM]),
                                      ALU.mult).then_inc(normalized[k], 1)
            for k in range(2):
                dve.wait_ge(g_turned[k], NORM_CHUNKS // 2)

            ATT_STEPS = 3 * PARTS + 2 * (PARTS - 1) + 7

            def steps_of(g):
                n = [0]

                def step(instruction):
                    n[0] += 1
                    instruction.then_inc(att_step, 1)
                    dve.wait_ge(att_step, g * ATT_STEPS + n[0])
                return step, n

            def add_part(g, parity, x, step):
                if x == 0:
                    dve.wait_ge(head_in[parity], (g - parity) * (8 * PART) + 16 * PART)
                else:
                    dve.wait_ge(body_in[x - 1], g * (16 * PART) + 16 * PART)
                rows_of = seq_part(parity, x).rearrange("p l d -> p d l")
                if x == 0:
                    step(dve.tensor_reduce(sess_sum, rows_of, AX.X, ALU.add))
                    return
                step(dve.tensor_reduce(part_sum, rows_of, AX.X, ALU.add))
                if x < PARTS - 1:
                    step(dve.tensor_tensor(sess_sum, sess_sum, part_sum, ALU.add))
                else:
                    dve.tensor_tensor(sess_sum, sess_sum, part_sum, ALU.add).then_inc(sess_summed, 1)

            def attend(g, parity, step, n):
                mean = 1.0 / (LAYERS + 1)
                dve.wait_ge(sess_turned, g + 1)
                dve.tensor_scalar(turned, sess_t_ps, mean, None, ALU.mult).then_inc(sess_placed, 1)
                dve.wait_ge(qk_made, g + 1)
                step(dve.tensor_copy(qk, qk_ps))
                for x in range(PARTS):
                    step(dve.tensor_tensor(prod, seq_part(parity, x), qk[:, None, 0:DIM].to_broadcast([P, PART, DIM]),
                                           ALU.mult))
                    step(dve.tensor_reduce(att[:, x * PART:(x + 1) * PART], prod, AX.X, ALU.add))
                step(dve.tensor_scalar(att, att, mean, qk[:, DIM:DIM + 1], ALU.mult, ALU.add))
                step(dve.tensor_reduce(tiny[:, 2:3], att, AX.X, ALU.max))
                dve.tensor_scalar(tiny[:, 0:1], tiny[:, 2:3], -float(DIM) ** -0.5, None, ALU.mult).then_inc(att_made, 1)
                dve.wait_ge(exp_made, g + 1)
                step(dve.reciprocal(tiny[:, 5:6], tiny[:, 1:2]))
                step(dve.tensor_scalar(prob, prob, tiny[:, 5:6], None, ALU.mult))
                for x in range(PARTS):
                    rows_of = seq_part(parity, x)
                    step(dve.tensor_tensor(rows_of, rows_of, prob[:, x * PART:(x + 1) * PART, None].to_broadcast(
                        [P, PART, DIM]), ALU.mult))
                    half = rows_of[:, 0:PART // 2, :]
                    dve.tensor_tensor(half, half, rows_of[:, PART // 2:PART, :], ALU.add).then_inc(seq_weighted, 1)
                dve.wait_ge(seq_mixed, g * PARTS + PARTS)
                dve.tensor_scalar(turned, mix_ps, mean, None, ALU.mult).then_inc(mix_placed, 1)
                dve.wait_ge(emb_rooted, g + 1)
                step(dve.tensor_scalar(tiny[:, 6:7], tiny[:, 4:5], EPS, None, ALU.max))
                step(dve.reciprocal(tiny[:, 7:8], tiny[:, 6:7]))
                dve.tensor_scalar(select, emb_ps, tiny[:, 7:8], W_K, ALU.mult, ALU.mult).then_inc(selected, 1)
                dve.wait_ge(select_turned, g + 1)
                dve.tensor_copy(select_t[parity], select_ps).then_inc(select_placed, 1)
                assert n[0] == ATT_STEPS, n[0]

            def take(g, i):
                dve.wait_ge(scored[1], uses_before(1, g, i) + 1)
                wait_past(dve, stored[1], uses_before(1, g, i) * 16)
                dve.tensor_copy(out_stage[1], pair(1)).then_inc(taken[1], 1)

            def scores_of(g, parity, more):
                step, n = steps_of(g + 1)
                for i in range(MEET):
                    take(g, i)
                    if more and i in SUM_AFTER:
                        add_part(g + 1, 1 - parity, SUM_AFTER[i], step)
                if more:
                    add_part(g + 1, 1 - parity, PARTS - 1, step)
                    attend(g + 1, 1 - parity, step, n)

            step, n = steps_of(0)
            for x in range(PARTS):
                add_part(0, 0, x, step)
            attend(0, 0, step, n)
            all_groups(dve, scores_of)


def kernel(**inputs):
    import numpy as np
    import concourse.bacc as bacc
    from concourse.bass_utils import run_bass_kernel_spmd as run

    def flat(x):
        return np.ascontiguousarray(x)

    emb = np.zeros((TABLE_ROWS, DIM), np.float32)
    emb[:N_NODES] = inputs["L0_rec_item_emb"]
    adj = np.asarray(inputs["L0_rec_adj_indices"])
    edges = np.zeros((2, P * COLS), adj.dtype)
    edges[0] = N_NODES - 1
    edges[:, :N_EDGES] = adj
    val = np.zeros(P * COLS, np.float32)
    val[:N_EDGES] = inputs["L0_rec_adj_values"]
    arrays = {
        "emb": emb,
        "edge_src": flat(edges[1].reshape(P, COLS)),
        "edge_dst": flat(edges[0].reshape(P, COLS)),
        "edge_val": val.reshape(P, COLS),
        "items": flat(inputs["r_items"]),
        "alias": flat(inputs["r_alias_inputs"]),
        "wq_t": flat(np.asarray(inputs["L0_rec_Wq"]).T),
        "bq": flat(np.asarray(inputs["L0_rec_bq"]).reshape(DIM, 1)),
        "wk": flat(inputs["L0_rec_Wk"]),
        "bk": flat(np.asarray(inputs["L0_rec_bk"]).reshape(DIM, 1)),
        "wv_t": flat(np.asarray(inputs["L0_rec_Wv"]).T),
        "bv": flat(np.asarray(inputs["L0_rec_bv"]).reshape(1, DIM)),
    }
    nc = bacc.Bacc("TRN2", target_bir_lowering=False, num_devices=1)
    named = {f"in_{k}": v for k, v in arrays.items()}
    args = [nc.dram_tensor(k, v.shape, mybir.dt.from_np(v.dtype), kind="ExternalInput").ap()
            for k, v in named.items()]
    args.append(nc.dram_tensor("out_scores", [SESSIONS, N_NODES], F32, kind="ExternalOutput").ap())
    bass_graph_session_scores(nc, *args)
    r = run(nc, [named], core_ids=[0])
    return r.results[0]["out_scores"]
```
